# Optimizing a Trainium2 kernel written in Bass

```python
import numpy as np
import jax
import jax.numpy as jnp

def _softmax(x, axis=-1):
    return jax.nn.softmax(x, axis=axis)

def _gelu(x):
    return jax.nn.gelu(x, approximate=True)

def _silu(x):
    return jax.nn.silu(x)

def _sigmoid(x):
    return jax.nn.sigmoid(x)

def _layernorm(x, axis=-1, eps=1e-05):
    m = jnp.mean(x, axis=axis, keepdims=True)
    v = jnp.var(x, axis=axis, keepdims=True)
    return (x - m) / jnp.sqrt(v + eps)

def _scatter_add(tgt, idx, src, axis=0):
    return tgt.at[idx].add(src)

def _segment_sum(src, seg, n):
    return jax.ops.segment_sum(src, seg, n)
kernel_name = 'mk_gnn_preln_d4_gnn_r64_4d29ee'

def setup_inputs(seed: int=0):
    np.random.seed(seed)
    _w = jnp.asarray

    def _rec_inputs():
        import jax
        import jax.numpy as jnp
        _gk = jax.random.key(seed)
        x = -0.000202 + 1 * jax.random.normal(jax.random.fold_in(_gk, 1), (100000, 64), jnp.float32)
        src = jax.random.randint(jax.random.fold_in(_gk, 2), (50000,), 0, 100000, jnp.int32)
        dst = jax.random.randint(jax.random.fold_in(_gk, 3), (50000,), 0, 100000, jnp.int32)
        _o = jnp.argsort(dst, stable=True)
        src = src[_o]
        dst = dst[_o]
        edge_type_8 = jax.random.randint(jax.random.fold_in(_gk, 13), (50000,), 0, 8, jnp.int32)
        edge_weight = jax.random.uniform(jax.random.fold_in(_gk, 14), (50000,), jnp.float32, 0.0, 1)
        return (x, src, dst, edge_type_8, edge_weight)
    x, src, dst, edge_type_8, edge_weight = _rec_inputs()

    def _L0_gnn_setup():
        import jax, jax.numpy as jnp
        import numpy as np
        N_NODES = 100000
        N_EDGES = 1250000
        D_IN = 64
        D_H = 64

        def _sage_layer(h, W_self, W_neigh, b, src, dst, deg_inv):
            neigh_sum = jax.ops.segment_sum(h[src], dst, num_segments=N_NODES)
            neigh = neigh_sum * deg_inv[:, None]
            return h @ W_self + neigh @ W_neigh + b
        key = jax.random.key(seed)
        ks = jax.random.split(key, 10)
        x = jax.random.normal(ks[0], (N_NODES, D_IN), dtype=jnp.float32)
        src = jax.random.randint(ks[1], (N_EDGES,), 0, N_NODES, dtype=jnp.int64 if jax.config.read('jax_enable_x64') else jnp.int32)
        dst = jax.random.randint(ks[2], (N_EDGES,), 0, N_NODES, dtype=jnp.int64 if jax.config.read('jax_enable_x64') else jnp.int32)
        s = 1.0 / np.sqrt(D_IN)
        W_self0 = jax.random.uniform(ks[3], (D_IN, D_H), jnp.float32, -s, s)
        W_neigh0 = jax.random.uniform(ks[4], (D_IN, D_H), jnp.float32, -s, s)
        b0 = jnp.zeros((D_H,), jnp.float32)
        s2 = 1.0 / np.sqrt(D_H)
        W_self1 = jax.random.uniform(ks[5], (D_H, D_H), jnp.float32, -s2, s2)
        W_neigh1 = jax.random.uniform(ks[6], (D_H, D_H), jnp.float32, -s2, s2)
        b1 = jnp.zeros((D_H,), jnp.float32)
        return {'x': x, 'W_self0': W_self0, 'W_neigh0': W_neigh0, 'b0': b0, 'W_self1': W_self1, 'W_neigh1': W_neigh1, 'b1': b1, 'src': src, 'dst': dst}
    _L0_gnn_all = _L0_gnn_setup()
    _L0_gnn_in = {k: v for k, v in _L0_gnn_all.items() if k in ('W_self0', 'W_neigh0', 'b0', 'W_self1', 'W_neigh1', 'b1')}
    del _L0_gnn_all

    def _L1_gnn_setup():
        import jax, jax.numpy as jnp
        import numpy as np
        N_NODES = 100000
        key = jax.random.key(seed)
        k1, k2 = jax.random.split(key)
        x = jax.random.normal(k1, (N_NODES, 64), dtype=jnp.float32)
        edge_index = jax.random.randint(k2, (2, 25000), 0, N_NODES, dtype=jnp.int64)
        return {'x': x, 'edge_index': edge_index}
    _L1_gnn_all = _L1_gnn_setup()
    _L1_gnn_in = {k: v for k, v in _L1_gnn_all.items() if k in ()}
    del _L1_gnn_all

    def _L2_gnn_setup():
        import jax, jax.numpy as jnp
        import numpy as np
        N_NODES = 100000
        N_EDGES = 18750
        D_IN = 64
        D_OUT = 64
        N_REL = 8
        key = jax.random.key(seed)
        k1, k2, k3, k4, k5 = jax.random.split(key, 5)
        x = jax.random.normal(k1, (N_NODES, D_IN), dtype=jnp.float32)
        edge_index = jax.random.randint(k2, (2, N_EDGES), 0, N_NODES, dtype=jnp.int32)
        edge_type = jax.random.randint(k3, (N_EDGES,), 0, N_REL, dtype=jnp.int32)
        wb = float(np.sqrt(6.0 / (D_IN + D_OUT)))
        weight = jax.random.uniform(k4, (N_REL, D_IN, D_OUT), dtype=jnp.float32, minval=-wb, maxval=wb)
        self_loop_w = jax.random.uniform(k5, (D_OUT, D_IN), dtype=jnp.float32, minval=-wb, maxval=wb)
        return {'x': x, 'edge_index': edge_index, 'edge_type': edge_type, 'weight': weight, 'self_loop_w': self_loop_w}
    _L2_gnn_all = _L2_gnn_setup()
    _L2_gnn_in = {k: v for k, v in _L2_gnn_all.items() if k in ('weight', 'self_loop_w')}
    del _L2_gnn_all

    def _L3_gnn_setup():
        import jax, jax.numpy as jnp
        import numpy as np
        N, F, E = (50000, 64, 1250000)
        key = jax.random.key(seed)
        k1, k2, k3 = jax.random.split(key, 3)
        x = jax.random.normal(k1, (N, F), dtype=jnp.float32)
        edge_weight = jax.random.uniform(k2, (E,), dtype=jnp.float32)
        edge_index = jax.random.randint(k3, (2, E), 0, N, dtype=jnp.int64)
        return {'x': x, 'edge_weight': edge_weight, 'edge_index': edge_index}
    _L3_gnn_all = _L3_gnn_setup()
    _L3_gnn_in = {k: v for k, v in _L3_gnn_all.items() if k in ()}
    del _L3_gnn_all
    return {'x': x, 'src': src, 'dst': dst, 'edge_type_8': edge_type_8, 'edge_weight': edge_weight, 'L0_gnn_W_self0': _L0_gnn_in['W_self0'], 'L0_gnn_W_neigh0': _L0_gnn_in['W_neigh0'], 'L0_gnn_b0': _L0_gnn_in['b0'], 'L0_gnn_W_self1': _L0_gnn_in['W_self1'], 'L0_gnn_W_neigh1': _L0_gnn_in['W_neigh1'], 'L0_gnn_b1': _L0_gnn_in['b1'], 'L2_gnn_weight': _L2_gnn_in['weight'], 'L2_gnn_self_loop_w': _L2_gnn_in['self_loop_w']}

def reference(x, src, dst, edge_type_8, edge_weight, L0_gnn_W_self0, L0_gnn_W_neigh0, L0_gnn_b0, L0_gnn_W_self1, L0_gnn_W_neigh1, L0_gnn_b1, L2_gnn_weight, L2_gnn_self_loop_w):
    import jax
    import jax.numpy as jnp

    def _L0_gnn_ref(x, W_self0, W_neigh0, b0, W_self1, W_neigh1, b1, src, dst):
        import jax, jax.numpy as jnp
        import numpy as np
        N_NODES = 100000
        N_EDGES = 1250000
        D_IN = 64
        D_H = 64

        def _sage_layer(h, W_self, W_neigh, b, src, dst, deg_inv):
            neigh_sum = jax.ops.segment_sum(h[src], dst, num_segments=N_NODES)
            neigh = neigh_sum * deg_inv[:, None]
            return h @ W_self + neigh @ W_neigh + b
        deg = jax.ops.segment_sum(jnp.ones_like(dst, dtype=jnp.float32), dst, num_segments=N_NODES)
        deg_inv = 1.0 / jnp.maximum(deg, 1.0)
        h = _sage_layer(x, W_self0, W_neigh0, b0, src, dst, deg_inv)
        h = jax.nn.relu(h)
        h = _sage_layer(h, W_self1, W_neigh1, b1, src, dst, deg_inv)
        h = jax.nn.relu(h)
        return h

    def _L1_gnn_ref(x, edge_index):
        import jax, jax.numpy as jnp
        import numpy as np
        N_NODES = 100000
        dst, src = (edge_index[0], edge_index[1])
        msgs = x[src]
        out = jax.ops.segment_sum(msgs, dst, num_segments=x.shape[0])
        return out

    def _L2_gnn_ref(x, edge_index, edge_type, weight, self_loop_w):
        import jax, jax.numpy as jnp
        import numpy as np
        N_NODES = 100000
        N_EDGES = 18750
        D_IN = 64
        D_OUT = 64
        N_REL = 8
        num_nodes = x.shape[0]
        num_relations = weight.shape[0]
        src, dst = (edge_index[0], edge_index[1])
        x_src = x[src]
        out = jnp.zeros((num_nodes, weight.shape[2]), dtype=x.dtype)
        for r in range(num_relations):
            mask = (edge_type == r)[:, None]
            msg = jnp.where(mask, x_src @ weight[r], 0.0)
            out = out + jax.ops.segment_sum(msg, dst, num_segments=num_nodes)
        out = out + x @ self_loop_w.T
        return jax.nn.relu(out)

    def _L3_gnn_ref(x, edge_weight, edge_index):
        import jax, jax.numpy as jnp
        import numpy as np
        N, F, E = (50000, 64, 1250000)
        src = edge_index[0]
        dst = edge_index[1]
        msg = x[src] * edge_weight[:, None]
        out = jax.ops.segment_sum(msg, dst, num_segments=x.shape[0])
        return out
    edge_index = jnp.stack([src, dst])
    h = jnp.maximum(_layernorm(x, axis=-1), 0.0)
    x = x + _L0_gnn_ref(h, L0_gnn_W_self0, L0_gnn_W_neigh0, L0_gnn_b0, L0_gnn_W_self1, L0_gnn_W_neigh1, L0_gnn_b1, src, dst)
    h = jnp.maximum(_layernorm(x, axis=-1), 0.0)
    x = x + _L1_gnn_ref(h, edge_index)
    h = jnp.maximum(_layernorm(x, axis=-1), 0.0)
    x = x + _L2_gnn_ref(h, edge_index, edge_type_8, L2_gnn_weight, L2_gnn_self_loop_w)
    h = jnp.maximum(_layernorm(x, axis=-1), 0.0)
    x = x + _L3_gnn_ref(h, edge_weight, edge_index)
    return x

_drawn_inputs = setup_inputs


def setup_inputs(seed=0):
    import zlib

    import numpy as np

    out = dict(_drawn_inputs(seed))
    spreads = {'L0_gnn_b0': (0.0, 0.1), 'L0_gnn_b1': (0.0, 0.1)}
    factors = {}
    for name, (base, spread) in spreads.items():
        noise = np.random.default_rng([zlib.crc32(name.encode()), seed]).standard_normal(out[name].shape)
        drawn = base * np.exp(spread * noise) if base else spread * noise
        out[name] = jnp.asarray(drawn.astype(out[name].dtype))
    for name, factor in factors.items():
        out[name] = (out[name] * factor).astype(out[name].dtype)
    return out
```

```python
import concourse.bass as bass
import numpy as np
from concourse import mybir
from contextlib import ExitStack

N, D, E, REL = 100000, 64, 50000, 8
C, K, U = 4, 3, 4
BLK, CAP, W = 128 * C, 128 * K, C * D
NB = -(-N // BLK)
NROWS = (NB + 1) * BLK
T = -(-E // 128)
CH = 14
T = -(-T // (2 * CH)) * 2 * CH
LEAD = 3
SMAX = NB + E // CAP
ITERS = -(-SMAX // U)
SROOM = (ITERS + 1) * U
J = -(-SROOM // 128)
PW = 5
TRASH = SROOM * CAP
TROWS = TRASH + 256
PC = 16
NP = NB * BLK // (128 * PC)
EPS = 1e-5
ROUND = float(3 << 22)
fp32, i32 = mybir.dt.float32, mybir.dt.int32
ALU, ACT, AX = mybir.AluOpType, mybir.ActivationFunctionType, mybir.AxisListType
assert TROWS * PW % 128 == 0 and NB * BLK % (128 * PC) == 0 and 128 * T - E <= 256 and NB + 1 >= 128


def tensors(nc, ctx):
    def sb(name, shape, dt=fp32):
        return ctx.enter_context(nc.sbuf_tensor(name, shape, dt))

    def ps(name, shape):
        return ctx.enter_context(nc.psum_tensor(name, shape, fp32))

    sems = []

    def clear():
        nc.clear_and_free_semaphores(sems)
        nc.all_engine_barrier()

    ctx.callback(clear)

    def sem(name):
        sems.append(nc.alloc_semaphore(name))
        return sems[-1]

    return sb, ps, sem


def place_edges(nc, io, keepers):
    with ExitStack() as ctx:
        sb, ps, sem = tensors(nc, ctx)
        iota, ident, eps = keepers["iota"], keepers["ident"], keepers["eps"]
        keep, ids, iters = keepers["keep"], keepers["ids"], keepers["iters"]
        iota_i = sb("iota_i", [128, NB + 1], i32)
        pidx_i = sb("pidx_i", [128, J], i32)
        pidx = sb("pidx", [128, J])
        tri, ones = sb("tri", [128, 128]), sb("ones", [128, NB + 1])
        raw = [sb("dst_raw", [128, T], i32), sb("src_raw", [128, T], i32)]
        typ, wgt = sb("typ", [128, T], i32), sb("wgt", [128, T])
        tmp_i = sb("tmp_i", [128, 3, T], i32)
        blk = [sb(f"blk{a}", [128, T]) for a in range(2)]
        load = [sb(f"load{a}", [128, T, PW]) for a in range(2)]
        cur = [sb(f"cur{a}", [128, NB + 1]) for a in range(2)]
        pos = [sb(f"pos{a}", [128, T]) for a in range(2)]
        junk = [sb(f"junk{a}", [128, NB + 1]) for a in range(2)]
        nst, start = sb("nst", [128, NB]), sb("start", [128, NB])
        scan = [sb(f"scan{k}", [128, NB]) for k in range(2)]
        cols = sb("cols", [128, 3, J])
        diag = sb("diag", [128, 3 * J, 128])
        it_i = sb("it_i", [128, 1], i32)
        nothing = sb("nothing", [128, TROWS * PW // 128])
        ring_load = sb("ring_load", [128, 2, CH, PW])
        ring_pos = sb("ring_pos", [128, 2, CH], i32)
        px, pc_, psq, ph = (sb(n, [128, 2, PC, D]) for n in ("px", "pxc", "psq", "ph"))
        pst = sb("pst", [128, 2, 4, PC])
        tot = [ps(f"tot{a}", [128, 512]) for a in range(2)]
        rows = [ps(f"rows{k}", [128, 512]) for k in range(J)]

        iota_made, loaded, filled = sem("iota_made"), sem("edges_loaded"), sem("tables_filled")
        fill_made, order = sem("fill_made"), sem("vector_order")
        hist, hist_done = [sem(f"hist{a}") for a in range(2)], sem("hist_done")
        tot_done, diag_done, rows_done = sem("tot_done"), sem("diag_done"), sem("rows_done")
        ranked = [sem(f"ranked{a}") for a in range(2)]
        ring_made, ring_sent = [sem(f"ring_made{k}") for k in range(2)], [sem(f"ring_sent{k}") for k in range(2)]
        slot_taken = sem("slot_taken")
        x_in = [sem(f"x_in{k}") for k in range(2)]
        h_out = [sem(f"h_out{k}") for k in range(2)]
        centred, squared, varied, rooted, normed, pord = (sem(n) for n in ("centred", "squared", "varied", "rooted", "normed", "norm_order"))
        block = ctx.enter_context(nc.Block())
        x_v = io["x"][0:NP * PC * 128, :].rearrange("(b p c) d -> b p (c d)", p=128, c=PC)
        h_v = io["H0"][0:NP * PC * 128, :].rearrange("(b p c) d -> b p (c d)", p=128, c=PC)

        @block.sync
        def _(sp):
            for raw_t, name in zip((*raw, typ, wgt), ("dst", "src", "etype", "ew")):
                sp.dma_start(raw_t[:, :], io[name].rearrange("(p t) -> p t", t=T)).then_inc(loaded, 16)
            sp.wait_ge(fill_made, 2)
            for a in range(2):
                sp.dma_start(io["tab"][a].rearrange("(p r) w -> p (r w)", p=128), nothing[:, :]).then_inc(filled, 16)

            def load_x(b, u, n):
                sp.dma_start(px[:, u, :, :].rearrange("p c d -> p (c d)"), x_v[b, :, :]).then_inc(x_in[u], 16)

            for b in range(2):
                load_x(b, b, 0)
            for b in range(2, NP):
                sp.wait_ge(centred, b - 1)
                load_x(b, b % 2, 0)

        @block.gpsimd
        def _(pool):
            nc.gpsimd.iota(iota_i[:, :], pattern=[[1, NB + 1]], base=0, channel_multiplier=0).then_inc(iota_made, 1)
            nc.gpsimd.iota(pidx_i[:, :], pattern=[[128, J]], base=0, channel_multiplier=1).then_inc(iota_made, 1)
            nc.gpsimd.memset(nothing[:, :], 0.0).then_inc(fill_made, 1)
            pool.wait_ge(fill_made, 1)
            nc.gpsimd.memset(nothing[:, :].rearrange("p (r w) -> p r w", w=PW)[:, :, 1:2], -1.0).then_inc(fill_made, 1)
            pool.wait_ge(filled, 32)

            def scatter(a, i):
                for u in range(2):
                    n = (T // (2 * CH)) * a + i
                    pool.wait_ge(ranked[a], (2 * i + u + 1) * CH)
                    pool.sem_inc(slot_taken, 1)
                    until(pool, ring_sent[u], n * 16 * CH)
                    nc.gpsimd.tensor_copy(ring_load[:, u, :, :].bitcast(i32),
                                          load[a][:, bass.ds((2 * i + u) * CH, CH), :].bitcast(i32)).then_inc(ring_made[u], 1)
                    nc.gpsimd.tensor_copy(ring_pos[:, u, :], pos[a][:, bass.ds((2 * i + u) * CH, CH)]).then_inc(ring_made[u], 1)
                    pool.wait_ge(ring_made[u], n * 2 + 2)
                    pool.sem_inc(slot_taken, 1)
                    for c in range(CH):
                        nc.gpsimd.indirect_dma_start(
                            out=io["tab"][a], out_offset=bass.IndirectOffsetOnAxis(ap=ring_pos[:, u, c:c + 1], axis=0),
                            in_=ring_load[:, u, c, :], in_offset=None).then_inc(ring_sent[u], 16)

            scatter(0, 0)
            for a in range(2):
                with pool.Fori(1 - a, T // (2 * CH)) as i:
                    scatter(a, i)
            for u in range(2):
                pool.wait_ge(ring_sent[u], 2 * (T // (2 * CH)) * 16 * CH)

        @block.tensor
        def _(pe):
            pe.wait_ge(hist_done, 1)
            for a in range(2):
                nc.tensor.matmul(tot[a][:, 0:NB + 1], ones[:, 0:128], cur[a][:, :], start=True, stop=True)
                nc.tensor.matmul(tot[a][:, 256:256 + NB + 1], tri[:, :], cur[a][:, :], start=True, stop=True).then_inc(tot_done, 1)
            for a in range(2):
                pe.wait_ge(diag_done, a + 1)
                for f in range(3):
                    for j in range(J):
                        mm = nc.tensor.matmul(rows[j][:, f * 128:(f + 1) * 128], ones[:, 0:128], diag[:, f * J + j, :], start=True, stop=True)
                mm.then_inc(rows_done, 1)

        @block.scalar
        def _(act):
            for b in range(NP):
                u = b % 2
                act.wait_ge(centred, b + 1)
                if b >= 2:
                    act.wait_ge(varied, b - 1)
                nc.scalar.activation(psq[:, u, :, :], pc_[:, u, :, :], ACT.Square).then_inc(squared, 1)
                act.wait_ge(varied, b + 1)
                nc.scalar.activation(pst[:, u, 2, :], pst[:, u, 1, :], ACT.Sqrt, bias=eps[:, :], scale=1.0 / D).then_inc(rooted, 1)
                act.wait_ge(normed, b + 1)
                act.dma_start(h_v[b, :, :], ph[:, u, :, :].rearrange("p c d -> p (c d)")).then_inc(h_out[u], 16)
            for u in range(2):
                act.wait_ge(h_out[u], 16 * len(range(u, NP, 2)))

        @block.vector
        def _(dve):
            count = [0]

            def link(ins):
                count[0] += 1
                ins.then_inc(order, 1)
                dve.wait_ge(order, count[0])

            v = nc.vector
            v.memset(ones[:, :], 1.0)
            v.memset(eps[:, :], EPS)
            for a in range(2):
                v.memset(cur[a][:, :], 0.0).then_inc(hist[a], 1)
            dve.wait_ge(iota_made, 2)
            v.tensor_copy(iota[:, :], iota_i[:, :])
            link(v.tensor_copy(pidx[:, :], pidx_i[:, :]))
            v.tensor_scalar(tri[:, :], iota[:, 0:128], pidx[:, 0:1], None, ALU.is_gt)
            v.tensor_scalar(ident[:, :], iota[:, 0:128], pidx[:, 0:1], None, ALU.is_equal)
            dve.wait_ge(loaded, 64)
            for a in range(2):
                v.tensor_scalar(tmp_i[:, 0, :], raw[a][:, :], BLK.bit_length() - 1, None, ALU.logical_shift_right)
                v.tensor_scalar(tmp_i[:, 1, :], raw[a][:, :], C.bit_length() - 1, 127, ALU.logical_shift_right, ALU.bitwise_and)
                link(v.tensor_scalar(tmp_i[:, 2, :], raw[a][:, :], C - 1, None, ALU.bitwise_and))
                v.tensor_copy(blk[a][:, :], tmp_i[:, 0, :])
                v.tensor_copy(load[a][:, :, 0].bitcast(i32), raw[1 - a][:, :])
                v.tensor_copy(load[a][:, :, 1], tmp_i[:, 1, :])
                v.tensor_copy(load[a][:, :, 2], tmp_i[:, 2, :])
                v.tensor_copy(load[a][:, :, 3], typ[:, :])
                link(v.tensor_copy(load[a][:, :, 4], wgt[:, :]))
            with dve.Fori(0, T // CH) as i:
                for c in range(CH):
                    for a in range(2):
                        dve.wait_ge(hist[a], i * CH + c + 1)
                        v.scalar_tensor_tensor(out=cur[a][:, :], in0=iota[:, :], scalar=blk[a][:, bass.ds(i * CH + c, 1)], in1=cur[a][:, :],
                                               op0=ALU.is_equal, op1=ALU.add).then_inc(hist[a], 1)
            for a in range(2):
                dve.wait_ge(hist[a], T + 1)
            v.memset(junk[0][:, :], 0.0).then_inc(hist_done, 1)
            for a in range(2):
                dve.wait_ge(tot_done, a + 1)
                link(v.tensor_scalar(nst[:, :], tot[a][:, 0:NB], 1.0 / CAP, 0.5 - 0.5 / CAP, ALU.mult, ALU.add))
                link(v.tensor_scalar(nst[:, :], nst[:, :], ROUND, ROUND, ALU.add, ALU.subtract))
                link(v.tensor_scalar(nst[:, :], nst[:, :], 1.0, None, ALU.max))
                link(v.tensor_copy(scan[0][:, :], nst[:, :]))
                s, k = 1, 0
                while s < NB:
                    v.tensor_copy(scan[1 - k][:, 0:s], scan[k][:, 0:s])
                    link(v.tensor_tensor(scan[1 - k][:, s:NB], scan[k][:, s:NB], scan[k][:, 0:NB - s], ALU.add))
                    s, k = 2 * s, 1 - k
                end = scan[k]
                link(v.tensor_tensor(start[:, :], end[:, :], nst[:, :], ALU.subtract))
                link(v.tensor_scalar(cur[a][:, 0:NB], start[:, :], float(CAP), None, ALU.mult))
                v.tensor_tensor(cur[a][:, 0:NB], cur[a][:, 0:NB], tot[a][:, 256:256 + NB], ALU.add)
                v.tensor_scalar(cur[a][:, NB:NB + 1], tot[a][:, 256 + NB:257 + NB], float(TRASH), None, ALU.add)
                for j in range(J):
                    for f, (row, op) in enumerate(((start, ALU.is_le), (start, ALU.is_equal), (end, ALU.is_equal))):
                        if f == 2:
                            link(v.tensor_scalar(pst[:, 0, 0, j:j + 1], pidx[:, j:j + 1], 1.0, None, ALU.add))
                        link(v.scalar_tensor_tensor(out=junk[0][:, 0:NB], in0=row[:, :], scalar=(pst[:, 0, 0, j:j + 1] if f == 2 else pidx[:, j:j + 1]),
                                                    in1=ones[:, 0:NB], op0=op, op1=ALU.mult, accum_out=cols[:, f, j:j + 1]))
                link(v.tensor_scalar(cols[:, 1, :], cols[:, 1, :], -1.0, 1.0, ALU.mult, ALU.add))
                link(v.tensor_scalar(cols[:, 0, :], cols[:, 0, :], 1.0, None, ALU.subtract))
                link(v.scalar_tensor_tensor(out=cols[:, 2, :], in0=cols[:, 0, :], scalar=float(-NB), in1=cols[:, 2, :], op0=ALU.add, op1=ALU.mult))
                link(v.tensor_scalar(cols[:, 2, :], cols[:, 2, :], float(NB), None, ALU.add))
                if a == 1:
                    dve.wait_ge(rows_done, 1)
                for f in range(3):
                    for j in range(J):
                        dg = v.tensor_scalar(diag[:, f * J + j, :], ident[:, :], cols[:, f, j:j + 1], None, ALU.mult)
                        if (f, j) == (2, J - 1):
                            dg.then_inc(diag_done, 1)
                link(v.tensor_copy(it_i[:, :], end[:, NB - 1:NB]))
                link(v.tensor_scalar(it_i[:, :], it_i[:, :], U - 1, None, ALU.add))
                link(v.tensor_scalar(iters[a][:, :], it_i[:, :], U.bit_length() - 1, None, ALU.logical_shift_right))
                dve.wait_ge(rows_done, a + 1)
                for j in range(J):
                    v.tensor_copy(ids[a][:, 0, j * 128:(j + 1) * 128], rows[j][:, 0:128])
                    v.tensor_copy(keep[a][:, j * 128:(j + 1) * 128], rows[j][:, 128:256])
                    link(v.tensor_copy(ids[a][:, 1, j * 128:(j + 1) * 128], rows[j][:, 256:384]))
            for a in range(2):
                with dve.Fori(0, T // CH) as i:
                    for c in range(CH):
                        col = i * CH + c
                        dve.wait_ge(hist[a], T + i * CH + c + 1)
                        v.scalar_tensor_tensor(out=junk[a][:, :], in0=iota[:, :], scalar=blk[a][:, bass.ds(col, 1)], in1=cur[a][:, :],
                                               op0=ALU.is_equal, op1=ALU.mult, accum_out=pos[a][:, bass.ds(col, 1)]).then_inc(ranked[a], 1)
                        v.scalar_tensor_tensor(out=cur[a][:, :], in0=iota[:, :], scalar=blk[a][:, bass.ds(col, 1)], in1=cur[a][:, :],
                                               op0=ALU.is_equal, op1=ALU.add).then_inc(hist[a], 1)
            n = 0

            def nl(ins):
                nonlocal n
                n += 1
                ins.then_inc(pord, 1)
                dve.wait_ge(pord, n)

            def last(b):
                u = b % 2
                dve.wait_ge(rooted, b + 1)
                nl(v.reciprocal(pst[:, u, 3, :], pst[:, u, 2, :]))
                if b >= 2:
                    dve.wait_ge(h_out[u], 16 * (b // 2))
                v.scalar_tensor_tensor(out=ph[:, u, :, :], in0=pc_[:, u, :, :], scalar=0.0,
                                       in1=pst[:, u, 3, :].unsqueeze(2).to_broadcast([128, PC, D]), op0=ALU.max, op1=ALU.mult).then_inc(normed, 1)

            for b in range(NP):
                u = b % 2
                dve.wait_ge(x_in[u], 16 * (b // 2 + 1))
                nl(v.tensor_reduce(pst[:, u, 0, :], px[:, u, :, :], AX.X, ALU.add))
                nl(v.tensor_scalar(pst[:, u, 0, :], pst[:, u, 0, :], -1.0 / D, None, ALU.mult))
                if b >= 2:
                    dve.wait_ge(normed, b - 1)
                v.tensor_tensor(pc_[:, u, :, :], px[:, u, :, :], pst[:, u, 0, :].unsqueeze(2).to_broadcast([128, PC, D]), ALU.add).then_inc(centred, 1)
                if b >= 1:
                    last(b - 1)
                dve.wait_ge(squared, b + 1)
                v.tensor_reduce(pst[:, u, 1, :], psq[:, u, :, :], AX.X, ALU.add).then_inc(varied, 1)
            last(NP - 1)


def until(eng, sem, count):
    if not (isinstance(count, int) and count <= 0):
        eng.wait_ge(sem, count)


def phase(nc, io, keepers, tag, a, rows_of, h_of, x_of, weights, bias, x_to, h_to,
          degrees=False, weighted=False, relational=False, norm=True):
    with ExitStack() as ctx:
        sb, ps, sem = tensors(nc, ctx)
        iota, ident, eps = keepers["iota"], keepers["ident"], keepers["eps"]
        keep, ids, iters, dinv = keepers["keep"][a], keepers["ids"][a], keepers["iters"][a], keepers["dinv"]
        sage = weights == "sage"
        own = weights is not None
        q = lambda name: f"{tag}_{name}"
        edges = sb(q("edges"), [128, U, K, PW])
        far = sb(q("far"), [128, U, K, D])
        place = sb(q("place"), [128, U, K, 128])
        chunk = sb(q("chunk"), [128, U, K, C])
        spread = sb(q("spread"), [128, U, K, W])
        agg = sb(q("agg"), [128, U, W])
        deg = sb(q("deg"), [128, U, C])
        mean = sb(q("mean"), [128, U, W])
        hb, xb = sb(q("hb"), [128, U, W]), sb(q("xb"), [128, U, W])
        turned = sb(q("turned"), [128, 2, 512])
        mix, xn, xc = sb(q("mix"), [128, U, W]), sb(q("xn"), [128, U, W]), sb(q("xc"), [128, U, W])
        sq, hn, st = sb(q("sq"), [128, U, W]), sb(q("hn"), [128, U, W]), sb(q("st"), [128, U, 4, C])
        ps_sum = [ps(q(f"ps_sum{k}"), [128, 512]) for k in range(2)]
        ps_turn = ps(q("ps_turn"), [128, 512])
        ps_mix = ps(q("ps_mix"), [128, 2, 512])
        if relational:
            kind = sb(q("kind"), [128, U, K, REL])
            by_kind = sb(q("by_kind"), [128, U, K, REL * D])
            kind_turned = sb(q("kind_turned"), [128, 2, 512])
            ps_kind = [ps(q(f"ps_kind{k}"), [128, 512]) for k in range(2)]
            ps_msg = ps(q("ps_msg"), [128, 512])

        S = lambda name: [sem(q(f"{name}{u}")) for u in range(U)]
        edges_in, far_in, block_in, stored = S("edges_in"), S("far_in"), S("block_in"), S("stored")
        hot, spread_made, summed, blocked = S("hot"), S("spread_made"), S("summed"), S("blocked")
        meaned, mixed_in, mixed = S("meaned"), S("product"), S("mixed")
        centred, squared, varied, rooted, normed = S("centred"), S("squared"), S("varied"), S("rooted"), S("normed")
        turn_made, turn_out = sem(q("turn_made")), sem(q("turn_out"))
        taken, primed = sem(q("slot_taken")), sem(q("primed"))
        order = S("order")
        if relational:
            kinds_made, kinds_turned, kinds_out, messages = sem(q("kinds_made")), sem(q("kinds_turned")), sem(q("kinds_out")), S("messages")
        block = ctx.enter_context(nc.Block())

        def view(t):
            return t.rearrange("(b p c) d -> b p (c d)", p=128, c=C)

        def steps(eng, stages):
            for n in range(-LEAD, U):
                for stage, lead in stages:
                    if n + lead >= 0:
                        stage(n + lead, (n + lead) % U, (n + lead) // U)
            with eng.Fori(1, eng.value_load(iters[0:1, 0:1], min_val=1, max_val=ITERS)) as i:
                for u in range(U):
                    for stage, lead in stages:
                        stage(i * U + (u + lead), (u + lead) % U, i + (u + lead) // U)

        def land(eng, sems, per_use, lead):
            count = eng.value_load(iters[0:1, 0:1], min_val=1, max_val=ITERS)
            for u in range(U):
                eng.wait_ge(sems[u], (count + 1 if u < lead else count) * 16 * per_use)
                eng.sem_inc(taken, 1)

        n_in = int(own) + int(x_of is not None)
        n_out = int(x_to is not None) + int(h_to is not None)

        @block.sync
        def _(sp):
            def fetch(n, u, r):
                until(sp, spread_made[u], r)
                sp.dma_start(edges[:, u, :, :].rearrange("p k w -> p (k w)"),
                             io["tab"][a][bass.ds(n * CAP, CAP), :].rearrange("(p k) w -> p (k w)", k=K)).then_inc(edges_in[u], 16)
                b = sp.value_load(ids[0:1, 0, bass.ds(n, 1)], min_val=0, max_val=NB - 1)
                until(sp, mixed[u], r)
                for t, dst in ((h_of if own else None, hb), (x_of, xb)):
                    if t is not None:
                        sp.dma_start(dst[:, u, :], view(io[t])[bass.ds(b, 1), :, :].rearrange("b p w -> (b p) w")).then_inc(block_in[u], 16)

            steps(sp, [(fetch, LEAD)])
            land(sp, edges_in, 1, LEAD)
            land(sp, block_in, n_in, LEAD)

        @block.gpsimd
        def _(pool):
            def gather(n, u, r):
                until(pool, edges_in[u], r * 16 + 16)
                pool.sem_inc(taken, 1)
                until(pool, spread_made[u], r)
                pool.sem_inc(taken, 1)
                for k in range(K):
                    nc.gpsimd.indirect_dma_start(
                        out=far[:, u, k, :], out_offset=None, in_=io[rows_of][0:NB * BLK, :],
                        in_offset=bass.IndirectOffsetOnAxis(ap=edges[:, u, k, 0:1].bitcast(i32), axis=0)).then_inc(far_in[u], 16)

            steps(pool, [(gather, LEAD)])
            land(pool, far_in, K, LEAD)

        @block.tensor
        def _(pe):
            def message(n, u, r):
                if relational:
                    for k in range(K):
                        m = n * K + k
                        until(pe, kinds_made, n + 1)
                        if u * K + k >= 2 or not isinstance(n, int):
                            until(pe, kinds_out, m - 1)
                        for j in range(4):
                            t = nc.tensor.transpose(ps_kind[(u * K + k) % 2][:, j * 128:(j + 1) * 128], by_kind[:, u, k, j * 128:(j + 1) * 128], ident[:, :])
                        t.then_inc(kinds_turned, 1)
                        until(pe, kinds_out, m + 1)
                        if k == 0:
                            until(pe, spread_made[(u - 1) % U], r + 1 if u > 0 else r)
                        for j in range(4):
                            mm = nc.tensor.matmul(ps_msg[:, k * D:(k + 1) * D], kind_turned[:, (u * K + k) % 2, j * 128:(j + 1) * 128],
                                                  keepers["w_rel"][:, j, :], start=(j == 0), stop=(j == 3))
                    mm.then_inc(messages[u], 1)

            def front(n, u, r):
                until(pe, hot[u], (r + 1) * (2 if weighted else 1))
                until(pe, spread_made[u], r + 1)
                until(pe, blocked[(u - 2) % U], r if u < 2 else r + 1)
                p = ps_sum[u % 2]
                for k in range(K):
                    mm = nc.tensor.matmul(p[:, 0:W], place[:, u, k, :], spread[:, u, k, :], start=(k == 0), stop=(k == K - 1))
                if degrees:
                    for k in range(K):
                        mm = nc.tensor.matmul(p[:, W:W + C], place[:, u, k, :], chunk[:, u, k, :], start=(k == 0), stop=(k == K - 1))
                mm.then_inc(summed[u], 1)

            def turn(n, u, r):
                if not own:
                    return
                if sage:
                    until(pe, meaned[u], r + 1)
                until(pe, block_in[u], (r + 1) * 16 * n_in)
                until(pe, turn_out, n)
                srcs = ((mean, 0), (hb, 1)) if sage else ((hb, 1),)
                for t, s in srcs:
                    for j in range(2):
                        tr = nc.tensor.transpose(ps_turn[:, s * 256 + j * 128:s * 256 + (j + 1) * 128], t[:, u, j * 128:(j + 1) * 128], ident[:, :])
                tr.then_inc(turn_made, 1)

            def product(n, u, r):
                if not own:
                    return
                until(pe, turn_out, n + 1)
                until(pe, mixed[(u - 1) % U], r + 1 if u > 0 else r)
                w = keepers[weights]
                for c2 in range(C // 2):
                    for s in ((0, 1) if sage else (1,)):
                        for odd in range(2):
                            o = c2 * D
                            mm = nc.tensor.matmul(ps_mix[:, odd, o:o + D], turned[64 * odd:64 * odd + 64, u % 2, s * 256 + c2 * 128:s * 256 + (c2 + 1) * 128],
                                                  w[64 * odd:64 * odd + 64, s, :], start=(not sage or s == 0), stop=(s == 1))
                            if c2 == C // 2 - 1 and s == 1:
                                mm.then_inc(mixed_in[u], 1)

            if relational:
                steps(pe, [(message, LEAD), (turn, 2), (product, 2), (front, LEAD)])
            else:
                steps(pe, [(front, LEAD), (turn, 2), (product, 2)])

        @block.scalar
        def _(act):
            def squares(n, u, r):
                if norm:
                    until(act, centred[u], r + 1)
                    until(act, varied[u], r)
                    nc.scalar.activation(sq[:, u, :], xc[:, u, :], ACT.Square).then_inc(squared[u], 1)

            def root(n, u, r):
                if norm:
                    until(act, varied[u], r + 1)
                    nc.scalar.activation(st[:, u, 2, :], st[:, u, 1, :], ACT.Sqrt, bias=eps[:, :], scale=1.0 / D).then_inc(rooted[u], 1)

            def kinds(n, u, r):
                if relational:
                    for k in range(K):
                        m = n * K + k
                        until(act, kinds_turned, m + 1)
                        nc.scalar.activation(kind_turned[:, (u * K + k) % 2, :], ps_kind[(u * K + k) % 2][:, :], ACT.Copy).then_inc(kinds_out, 1)

            def evacuate(n, u, r):
                if own:
                    until(act, turn_made, n + 1)
                    part = slice(0, 512) if sage else slice(256, 512)
                    nc.scalar.activation(turned[:, u % 2, part], ps_turn[:, part], ACT.Copy).then_inc(turn_out, 1)

            def activate(n, u, r):
                if tag == "A":
                    until(act, mixed[u], r + 1)
                    until(act, stored[u], r * 16 * n_out)
                    nc.scalar.activation(hn[:, u, :], mix[:, u, :], ACT.Relu).then_inc(normed[u], 1)

            def store(n, u, r):
                b = act.value_load(ids[0:1, 1, bass.ds(n, 1)], min_val=0, max_val=NB)
                until(act, normed[u] if norm or tag == "A" else mixed[u], r + 1)
                for t, src in ((x_to, xn), (h_to, hn)):
                    if t is not None:
                        act.dma_start(view(io[t])[bass.ds(b, 1), :, :].rearrange("b p w -> (b p) w"), src[:, u, :]).then_inc(stored[u], 16)

            steps(act, [(kinds, LEAD), (squares, 1), (root, 0), (evacuate, 2), (activate, 1), (store, 0)])
            land(act, stored, n_out, 0)

        @block.vector
        def _(dve):
            v = nc.vector
            v.memset(agg[:, U - 1, :], 0.0).then_inc(primed, 1)
            v.memset(deg[:, U - 1, :], 0.0).then_inc(primed, 1)

            def cd(ap):
                return ap.rearrange("p (c d) -> p c d", d=D)

            def wide(ap):
                return ap.unsqueeze(2).to_broadcast([128, C, D])

            def front(n, u, r):
                until(dve, edges_in[u], r * 16 + 16)
                until(dve, summed[u], r)
                v.tensor_tensor(place[:, u, :, :], edges[:, u, :, 1:2].to_broadcast([128, K, 128]),
                                iota[:, 0:128].unsqueeze(1).to_broadcast([128, K, 128]), ALU.is_equal)
                m = 2 if weighted else 1
                v.tensor_tensor(chunk[:, u, :, :], edges[:, u, :, 2:3].to_broadcast([128, K, C]),
                                iota[:, 0:C].unsqueeze(1).to_broadcast([128, K, C]), ALU.is_equal).then_inc(hot[u], 1)
                until(dve, hot[u], r * m + 1)
                if weighted:
                    v.tensor_tensor(chunk[:, u, :, :], chunk[:, u, :, :], edges[:, u, :, 4:5].to_broadcast([128, K, C]), ALU.mult).then_inc(hot[u], 1)
                    until(dve, hot[u], r * m + 2)
                if relational:
                    until(dve, far_in[u], (r + 1) * 16 * K)
                    v.tensor_tensor(kind[:, u, :, :], edges[:, u, :, 3:4].to_broadcast([128, K, REL]),
                                    iota[:, 0:REL].unsqueeze(1).to_broadcast([128, K, REL]), ALU.is_equal).then_inc(order[u], 1)
                    until(dve, order[u], r * ORD + 1)
                    for k in range(K):
                        bk = v.tensor_tensor(by_kind[:, u, k, :].rearrange("p (r d) -> p r d", d=D), far[:, u, k, :].unsqueeze(1).to_broadcast([128, REL, D]),
                                             kind[:, u, k, :].unsqueeze(2).to_broadcast([128, REL, D]), ALU.mult)
                    bk.then_inc(kinds_made, 1)

            def spreading(n, u, r):
                rows = far[:, u, :, :]
                until(dve, far_in[u], (r + 1) * 16 * K)
                if relational:
                    until(dve, messages[u], r + 1)
                    rows = ps_msg[:, 0:K * D].rearrange("p (k d) -> p k d", d=D)
                for k in range(K):
                    sp_ = v.tensor_tensor(cd(spread[:, u, k, :]), rows[:, k, :].unsqueeze(1).to_broadcast([128, C, D]),
                                          wide(chunk[:, u, k, :]), ALU.mult)
                sp_.then_inc(spread_made[u], 1)

            def order_of(u, r, k):
                until(dve, order[u], r * ORD + k)

            def add_up(n, u, r):
                o = int(relational)
                until(dve, summed[u], r + 1)
                until(dve, blocked[(u - 1) % U], r + 1 if u > 0 else r)
                if degrees:
                    v.scalar_tensor_tensor(out=deg[:, u, :], in0=deg[:, (u - 1) % U, :], scalar=keep[:, bass.ds(n, 1)],
                                           in1=ps_sum[u % 2][:, W:W + C], op0=ALU.mult, op1=ALU.add).then_inc(order[u], 1)
                v.scalar_tensor_tensor(out=agg[:, u, :], in0=agg[:, (u - 1) % U, :], scalar=keep[:, bass.ds(n, 1)],
                                       in1=ps_sum[u % 2][:, 0:W], op0=ALU.mult, op1=ALU.add).then_inc(blocked[u], 1)
                if degrees:
                    order_of(u, r, o + 1)
                    v.tensor_scalar(st[:, u, 3, :], deg[:, u, :], 1.0, None, ALU.max).then_inc(order[u], 1)
                    order_of(u, r, o + 2)
                    v.reciprocal(dinv[:, bass.ds(n, 1), :], st[:, u, 3, :].unsqueeze(1)).then_inc(order[u], 1)
                    order_of(u, r, o + 3)
                if sage:
                    until(dve, blocked[u], r + 1)
                    v.tensor_tensor(cd(mean[:, u, :]), cd(agg[:, u, :]), dinv[:, bass.ds(n, 1), :].rearrange("p a c -> p (a c)").unsqueeze(2).to_broadcast([128, C, D]),
                                    ALU.mult).then_inc(meaned[u], 1)

            def mixing(n, u, r):
                o = int(relational) + (3 if degrees else 0)
                until(dve, block_in[u], (r + 1) * 16 * n_in)
                until(dve, blocked[u], r + 1)
                if own:
                    until(dve, mixed_in[u], 2 * r + 2)
                    made = ps_mix[:, :, 0:W // 2].rearrange("p h (c d) -> p c h d", d=D)
                    four = lambda t: t[:, u, :].rearrange("p (c h d) -> p c h d", h=2, d=D)
                    if sage:
                        added = keepers[bias][:, :].unsqueeze(1).unsqueeze(1).to_broadcast([128, C // 2, 2, D])
                    if sage:
                        if tag == "A":
                            until(dve, normed[u], r)
                            v.tensor_tensor(four(mix), made, added, ALU.add).then_inc(mixed[u], 1)
                            return
                        v.tensor_tensor(four(mix), made, added, ALU.add).then_inc(order[u], 1)
                    else:
                        v.tensor_tensor(four(mix), made, four(agg), ALU.add).then_inc(order[u], 1)
                    order_of(u, r, o + 1)
                    until(dve, stored[u], r * 16 * n_out)
                    v.scalar_tensor_tensor(out=xn[:, u, :], in0=mix[:, u, :], scalar=0.0, in1=xb[:, u, :], op0=ALU.max, op1=ALU.add).then_inc(mixed[u], 1)
                else:
                    until(dve, stored[u], r * 16 * n_out)
                    v.tensor_tensor(xn[:, u, :], agg[:, u, :], xb[:, u, :], ALU.add).then_inc(mixed[u], 1)
                if norm:
                    o += int(own)
                    until(dve, mixed[u], r + 1)
                    v.tensor_reduce(st[:, u, 0, :], cd(xn[:, u, :]), AX.X, ALU.add).then_inc(order[u], 1)
                    order_of(u, r, o + 1)
                    v.tensor_scalar(st[:, u, 0, :], st[:, u, 0, :], -1.0 / D, None, ALU.mult).then_inc(order[u], 1)
                    order_of(u, r, o + 2)
                    v.tensor_tensor(cd(xc[:, u, :]), cd(xn[:, u, :]), wide(st[:, u, 0, :]), ALU.add).then_inc(centred[u], 1)

            def variance(n, u, r):
                if norm:
                    until(dve, squared[u], r + 1)
                    v.tensor_reduce(st[:, u, 1, :], cd(sq[:, u, :]), AX.X, ALU.add).then_inc(varied[u], 1)

            def last(n, u, r):
                if norm:
                    until(dve, rooted[u], r + 1)
                    v.reciprocal(st[:, u, 3, :], st[:, u, 2, :]).then_inc(order[u], 1)
                    order_of(u, r, ORD)
                    v.scalar_tensor_tensor(out=cd(hn[:, u, :]), in0=cd(xc[:, u, :]), scalar=0.0, in1=wide(st[:, u, 3, :]),
                                           op0=ALU.max, op1=ALU.mult).then_inc(normed[u], 1)

            ORD = int(relational) + 3 * int(degrees) + int(own and x_of is not None) + 3 * int(norm)
            until(dve, primed, 2)
            if relational:
                steps(dve, [(front, LEAD), (mixing, 1), (variance, 0), (add_up, 2), (last, 0), (spreading, LEAD)])
            else:
                steps(dve, [(front, LEAD), (spreading, LEAD), (mixing, 1), (variance, 0), (add_up, 2), (last, 0)])


def load_weights(nc, io, keepers):
    with ExitStack() as ctx:
        _, _, sem = tensors(nc, ctx)
        loaded = sem("weights_loaded")
        block = ctx.enter_context(nc.Block())

        @block.sync
        def _(sp):
            n = 0
            for name, dst in (("w_sage0", "sage0"), ("w_sage1", "sage1"), ("w_self", "own")):
                for half in range(2):
                    sp.dma_start(keepers[dst][64 * half:64 * half + 64, :, :], io[name].rearrange("s i o -> i s o")).then_inc(loaded, 16)
                    n += 1
            for j in range(REL // 2):
                for half in range(2):
                    sp.dma_start(keepers["w_rel"][64 * half:64 * half + 64, j, :], io["w_rel"][2 * j + half, :, :]).then_inc(loaded, 16)
                    n += 1
            for name in ("b0", "b1"):
                sp.dma_start(keepers[name][:, :], io[name].unsqueeze(0).to_broadcast([128, D])).then_inc(loaded, 16)
                n += 1
            sp.wait_ge(loaded, 16 * n)


def build(nc, io):
    with ExitStack() as ctx:
        def sb(name, shape, dt=fp32):
            return ctx.enter_context(nc.sbuf_tensor(name, shape, dt))

        for name in ("H0", "H1", "X1", "H3", "X2", "H4", "X3", "H5"):
            io[name] = nc.dram_tensor(name, (NROWS, D), fp32).ap()
        io["tab"] = [nc.dram_tensor(f"placed_{a}", (TROWS, PW), fp32).ap() for a in ("dst", "src")]
        keepers = {
            "iota": sb("iota", [128, NB + 1]), "ident": sb("ident", [128, 128]), "eps": sb("eps", [128, 1]),
            "keep": [sb(f"keep{a}", [128, J * 128]) for a in range(2)],
            "ids": [sb(f"ids{a}", [128, 2, J * 128], i32) for a in range(2)],
            "iters": [sb(f"iters{a}", [128, 1], i32) for a in range(2)],
            "dinv": sb("dinv", [128, J * 128, C]),
            "sage0": sb("w_sage0", [128, 2, D]), "sage1": sb("w_sage1", [128, 2, D]), "own": sb("w_own", [128, 2, D]),
            "w_rel": sb("w_rel", [128, REL // 2, D]), "b0": sb("b0", [128, D]), "b1": sb("b1", [128, D]),
        }
        load_weights(nc, io, keepers)
        place_edges(nc, io, keepers)
        run = lambda tag, wts, *args, **kw: phase(nc, io, {**keepers, "sage": keepers.get(wts)}, tag, args[0], args[1], args[2], args[3], "sage" if wts and wts != "own" else wts, *args[4:], **kw)
        run("A", "sage0", 0, "H0", "H0", None, "b0", None, "H1", degrees=True, norm=False)
        run("B", "sage1", 0, "H1", "H1", "x", "b1", "X1", "H3")
        run("C", None, 1, "H3", None, "X1", None, "X2", "H4")
        run("D", "own", 0, "H4", "H4", "X2", None, "X3", "H5", relational=True)
        run("E", None, 0, "H5", None, "X3", None, "out", None, weighted=True, norm=False)


def kernel(**inputs):
    import numpy as np
    import concourse.bacc as bacc
    from concourse.bass_utils import run_bass_kernel_spmd as run

    def padded(a, n, fill):
        out = np.full((n, *a.shape[1:]), fill, a.dtype)
        out[:len(a)] = a
        return out

    g = {k: np.asarray(v) for k, v in inputs.items()}
    arrays = {
        "x": padded(g["x"], NROWS, 0),
        "dst": padded(g["dst"].astype(np.int32), 128 * T, NB * BLK),
        "src": padded(g["src"].astype(np.int32), 128 * T, NB * BLK),
        "etype": padded(g["edge_type_8"].astype(np.int32), 128 * T, 0),
        "ew": padded(g["edge_weight"], 128 * T, 0),
        "w_sage0": np.stack([g["L0_gnn_W_neigh0"], g["L0_gnn_W_self0"]]),
        "w_sage1": np.stack([g["L0_gnn_W_neigh1"], g["L0_gnn_W_self1"]]),
        "w_self": np.ascontiguousarray(np.stack([g["L2_gnn_self_loop_w"].T, g["L2_gnn_self_loop_w"].T])),
        "w_rel": g["L2_gnn_weight"], "b0": g["L0_gnn_b0"], "b1": g["L0_gnn_b1"],
    }
    nc = bacc.Bacc("TRN2", target_bir_lowering=False, num_devices=1)
    io = {n: nc.dram_tensor(f"in_{n}", a.shape, i32 if a.dtype == np.int32 else fp32, kind="ExternalInput").ap() for n, a in arrays.items()}
    io["out"] = nc.dram_tensor("out_x", (NROWS, D), fp32, kind="ExternalOutput").ap()
    build(nc, io)
    r = run(nc, [{f"in_{n}": np.ascontiguousarray(a) for n, a in arrays.items()}], core_ids=[0])
    return r.results[0]["out_x"][:N]
```

```python
import concourse.bass as bass
import numpy as np
from concourse import mybir
from contextlib import ExitStack

N, D, E, REL = 100000, 64, 50000, 8
C, K, U = 4, 3, 4
BLK, CAP, W = 128 * C, 128 * K, C * D
NB = -(-N // BLK)
NROWS = (NB + 1) * BLK
T = -(-E // 128)
CH = 14
T = -(-T // (2 * CH)) * 2 * CH
LEAD = 8
SMAX = NB + E // CAP
ITERS = -(-SMAX // U)
SROOM = ITERS * U + -(-LEAD // U) * U
J = -(-SROOM // 128)
PW = 5
TRASH = SROOM * CAP
TROWS = TRASH + 256
PC = 16
NP = NB * BLK // (128 * PC)
EPS = 1e-5
ROUND = float(3 << 22)
fp32, i32, bf16 = mybir.dt.float32, mybir.dt.int32, mybir.dt.bfloat16
ALU, ACT, AX = mybir.AluOpType, mybir.ActivationFunctionType, mybir.AxisListType
assert TROWS * PW % 128 == 0 and NB * BLK % (128 * PC) == 0 and 128 * T - E <= 256 and NB + 1 >= 128


def tensors(nc, ctx):
    def sb(name, shape, dt=fp32):
        return ctx.enter_context(nc.sbuf_tensor(name, shape, dt))

    def ps(name, shape):
        return ctx.enter_context(nc.psum_tensor(name, shape, fp32))

    sems = []

    def clear():
        nc.clear_and_free_semaphores(sems)
        nc.all_engine_barrier()

    ctx.callback(clear)

    def sem(name):
        sems.append(nc.alloc_semaphore(name))
        return sems[-1]

    return sb, ps, sem


def place_edges(nc, io, keepers):
    with ExitStack() as ctx:
        sb, ps, sem = tensors(nc, ctx)
        iota, ident, eps = keepers["iota"], keepers["ident"], keepers["eps"]
        keep, fresh, ids, iters = keepers["keep"], keepers["fresh"], keepers["ids"], keepers["iters"]
        iota_i = sb("iota_i", [128, NB + 1], i32)
        pidx_i = sb("pidx_i", [128, J], i32)
        pidx = sb("pidx", [128, J])
        tri, ones = sb("tri", [128, 128]), sb("ones", [128, NB + 1])
        raw = [sb("dst_raw", [128, T], i32), sb("src_raw", [128, T], i32)]
        typ, wgt = sb("typ", [128, T], i32), sb("wgt", [128, T])
        tmp_i = sb("tmp_i", [128, 3, T], i32)
        blk = [sb(f"blk{a}", [128, T]) for a in range(2)]
        load = [sb(f"load{a}", [128, T, PW]) for a in range(2)]
        cur = [sb(f"cur{a}", [128, NB + 1]) for a in range(2)]
        pos = [sb(f"pos{a}", [128, T]) for a in range(2)]
        junk = [sb(f"junk{a}", [128, NB + 1]) for a in range(2)]
        nst, start = sb("nst", [128, NB]), sb("start", [128, NB])
        scan = [sb(f"scan{k}", [128, NB]) for k in range(2)]
        cols = sb("cols", [128, 3, J])
        diag = sb("diag", [128, 3 * J, 128])
        it_i = sb("it_i", [128, 1], i32)
        nothing = sb("nothing", [128, TROWS * PW // 128])
        ring_load = sb("ring_load", [128, 2, CH, PW])
        ring_pos = sb("ring_pos", [128, 2, CH], i32)
        px, pc_, psq, ph = (sb(n, [128, 2, PC, D]) for n in ("px", "pxc", "psq", "ph"))
        pst = sb("pst", [128, 2, 4, PC])
        tot = [ps(f"tot{a}", [128, 512]) for a in range(2)]
        rows = [ps(f"rows{k}", [128, 512]) for k in range(J)]

        iota_made, loaded, filled = sem("iota_made"), sem("edges_loaded"), sem("tables_filled")
        fill_made, order = sem("fill_made"), sem("vector_order")
        hist, hist_done = [sem(f"hist{a}") for a in range(2)], sem("hist_done")
        tot_done, diag_done, rows_done = sem("tot_done"), sem("diag_done"), sem("rows_done")
        ranked = [sem(f"ranked{a}") for a in range(2)]
        ring_made, ring_sent = [sem(f"ring_made{k}") for k in range(2)], [sem(f"ring_sent{k}") for k in range(2)]
        slot_taken = sem("slot_taken")
        x_in = [sem(f"x_in{k}") for k in range(2)]
        h_out = [sem(f"h_out{k}") for k in range(2)]
        centred, squared, varied, rooted, normed, pord = (sem(n) for n in ("centred", "squared", "varied", "rooted", "normed", "norm_order"))
        block = ctx.enter_context(nc.Block())
        x_v = io["x"][0:NP * PC * 128, :].rearrange("(b p c) d -> b p (c d)", p=128, c=PC)
        h_v = io["H0"][0:NP * PC * 128, :].rearrange("(b p c) d -> b p (c d)", p=128, c=PC)

        @block.sync
        def _(sp):
            for raw_t, name in zip((*raw, typ, wgt), ("dst", "src", "etype", "ew")):
                sp.dma_start(raw_t[:, :], io[name].rearrange("(p t) -> p t", t=T)).then_inc(loaded, 16)
            sp.wait_ge(fill_made, 2)
            for a in range(2):
                sp.dma_start(io["tab"][a].rearrange("(p r) w -> p (r w)", p=128), nothing[:, :]).then_inc(filled, 16)

            def load_x(b, u, n):
                sp.dma_start(px[:, u, :, :].rearrange("p c d -> p (c d)"), x_v[b, :, :]).then_inc(x_in[u], 16)

            for b in range(2):
                load_x(b, b, 0)
            for b in range(2, NP):
                sp.wait_ge(centred, b - 1)
                load_x(b, b % 2, 0)

        @block.gpsimd
        def _(pool):
            nc.gpsimd.iota(iota_i[:, :], pattern=[[1, NB + 1]], base=0, channel_multiplier=0).then_inc(iota_made, 1)
            nc.gpsimd.iota(pidx_i[:, :], pattern=[[128, J]], base=0, channel_multiplier=1).then_inc(iota_made, 1)
            nc.gpsimd.memset(nothing[:, :], 0.0).then_inc(fill_made, 1)
            pool.wait_ge(fill_made, 1)
            nc.gpsimd.memset(nothing[:, :].rearrange("p (r w) -> p r w", w=PW)[:, :, 1:2], 1.0).then_inc(fill_made, 1)
            pool.wait_ge(filled, 32)

            def scatter(a, i):
                for u in range(2):
                    n = (T // (2 * CH)) * a + i
                    pool.wait_ge(ranked[a], (2 * i + u + 1) * CH)
                    pool.sem_inc(slot_taken, 1)
                    until(pool, ring_sent[u], n * 16 * CH)
                    nc.gpsimd.tensor_copy(ring_load[:, u, :, :].bitcast(i32),
                                          load[a][:, bass.ds((2 * i + u) * CH, CH), :].bitcast(i32)).then_inc(ring_made[u], 1)
                    nc.gpsimd.tensor_copy(ring_pos[:, u, :], pos[a][:, bass.ds((2 * i + u) * CH, CH)]).then_inc(ring_made[u], 1)
                    pool.wait_ge(ring_made[u], n * 2 + 2)
                    pool.sem_inc(slot_taken, 1)
                    for c in range(CH):
                        nc.gpsimd.indirect_dma_start(
                            out=io["tab"][a], out_offset=bass.IndirectOffsetOnAxis(ap=ring_pos[:, u, c:c + 1], axis=0),
                            in_=ring_load[:, u, c, :], in_offset=None).then_inc(ring_sent[u], 16)

            scatter(0, 0)
            for a in range(2):
                with pool.Fori(1 - a, T // (2 * CH)) as i:
                    scatter(a, i)
            for u in range(2):
                pool.wait_ge(ring_sent[u], 2 * (T // (2 * CH)) * 16 * CH)

        @block.tensor
        def _(pe):
            for a in range(2):
                pe.wait_ge(hist_done, a + 1)
                nc.tensor.matmul(tot[a][:, 0:NB + 1], ones[:, 0:128], cur[a][:, :], start=True, stop=True)
                nc.tensor.matmul(tot[a][:, 256:256 + NB + 1], tri[:, :], cur[a][:, :], start=True, stop=True).then_inc(tot_done, 1)
                pe.wait_ge(diag_done, a + 1)
                for f in range(3):
                    for j in range(J):
                        mm = nc.tensor.matmul(rows[j][:, f * 128:(f + 1) * 128], ones[:, 0:128], diag[:, f * J + j, :], start=True, stop=True)
                mm.then_inc(rows_done, 1)

        @block.scalar
        def _(act):
            for b in range(NP):
                u = b % 2
                act.wait_ge(centred, b + 1)
                if b >= 2:
                    act.wait_ge(varied, b - 1)
                nc.scalar.activation(psq[:, u, :, :], pc_[:, u, :, :], ACT.Square).then_inc(squared, 1)
                act.wait_ge(varied, b + 1)
                nc.scalar.activation(pst[:, u, 2, :], pst[:, u, 1, :], ACT.Sqrt, bias=eps[:, :], scale=1.0 / D).then_inc(rooted, 1)
                act.wait_ge(normed, b + 1)
                act.dma_start(h_v[b, :, :], ph[:, u, :, :].rearrange("p c d -> p (c d)")).then_inc(h_out[u], 16)
            for u in range(2):
                act.wait_ge(h_out[u], 16 * len(range(u, NP, 2)))

        @block.vector
        def _(dve):
            count = [0]

            def link(ins):
                count[0] += 1
                ins.then_inc(order, 1)
                dve.wait_ge(order, count[0])

            v = nc.vector
            v.memset(ones[:, :], 1.0)
            v.memset(eps[:, :], EPS)
            for a in range(2):
                v.memset(cur[a][:, :], 0.0).then_inc(hist[a], 1)
            dve.wait_ge(iota_made, 2)
            v.tensor_copy(iota[:, :], iota_i[:, :])
            link(v.tensor_copy(pidx[:, :], pidx_i[:, :]))
            v.tensor_scalar(tri[:, :], iota[:, 0:128], pidx[:, 0:1], None, ALU.is_gt)
            v.tensor_scalar(ident[:, :], iota[:, 0:128], pidx[:, 0:1], None, ALU.is_equal)
            dve.wait_ge(loaded, 64)
            for a in range(2):
                v.tensor_scalar(tmp_i[:, 0, :], raw[a][:, :], BLK.bit_length() - 1, None, ALU.logical_shift_right)
                v.tensor_scalar(tmp_i[:, 1, :], raw[a][:, :], C.bit_length() - 1, 127, ALU.logical_shift_right, ALU.bitwise_and)
                link(v.tensor_scalar(tmp_i[:, 2, :], raw[a][:, :], C - 1, None, ALU.bitwise_and))
                v.tensor_copy(blk[a][:, :], tmp_i[:, 0, :])
                v.tensor_copy(load[a][:, :, 0].bitcast(i32), raw[1 - a][:, :])
                v.tensor_scalar(load[a][:, :, 1], tmp_i[:, 1, :], -1.0, None, ALU.mult)
                v.tensor_copy(load[a][:, :, 2], tmp_i[:, 2, :])
                v.tensor_copy(load[a][:, :, 3], typ[:, :])
                link(v.tensor_copy(load[a][:, :, 4], wgt[:, :]))
            def tally(a, col, seen):
                dve.wait_ge(hist[a], seen + 1)
                v.scalar_tensor_tensor(out=cur[a][:, :], in0=iota[:, :], scalar=blk[a][:, bass.ds(col, 1)], in1=cur[a][:, :],
                                       op0=ALU.is_equal, op1=ALU.add).then_inc(hist[a], 1)

            def rank(a, col):
                dve.wait_ge(hist[a], T + 1 + col)
                v.scalar_tensor_tensor(out=junk[a][:, :], in0=iota[:, :], scalar=blk[a][:, bass.ds(col, 1)], in1=cur[a][:, :],
                                       op0=ALU.is_equal, op1=ALU.mult, accum_out=pos[a][:, bass.ds(col, 1)]).then_inc(ranked[a], 1)

            def starts(a):
                dve.wait_ge(tot_done, a + 1)
                link(v.tensor_scalar(nst[:, :], tot[a][:, 0:NB], 1.0 / CAP, 0.5 - 0.5 / CAP, ALU.mult, ALU.add))
                link(v.tensor_scalar(nst[:, :], nst[:, :], ROUND, ROUND, ALU.add, ALU.subtract))
                link(v.tensor_scalar(nst[:, :], nst[:, :], 1.0, None, ALU.max))
                link(v.tensor_copy(scan[0][:, :], nst[:, :]))
                s, k = 1, 0
                while s < NB:
                    v.tensor_copy(scan[1 - k][:, 0:s], scan[k][:, 0:s])
                    link(v.tensor_tensor(scan[1 - k][:, s:NB], scan[k][:, s:NB], scan[k][:, 0:NB - s], ALU.add))
                    s, k = 2 * s, 1 - k
                end = scan[k]
                link(v.tensor_tensor(start[:, :], end[:, :], nst[:, :], ALU.subtract))
                link(v.tensor_scalar(cur[a][:, 0:NB], start[:, :], float(CAP), None, ALU.mult))
                v.tensor_tensor(cur[a][:, 0:NB], cur[a][:, 0:NB], tot[a][:, 256:256 + NB], ALU.add)
                v.tensor_scalar(cur[a][:, NB:NB + 1], tot[a][:, 256 + NB:257 + NB], float(TRASH), None, ALU.add)
                for j in range(J):
                    for f, (row, op) in enumerate(((start, ALU.is_le), (start, ALU.is_equal), (end, ALU.is_equal))):
                        if f == 2:
                            link(v.tensor_scalar(pst[:, 0, 0, j:j + 1], pidx[:, j:j + 1], 1.0, None, ALU.add))
                        link(v.scalar_tensor_tensor(out=junk[0][:, 0:NB], in0=row[:, :], scalar=(pst[:, 0, 0, j:j + 1] if f == 2 else pidx[:, j:j + 1]),
                                                    in1=ones[:, 0:NB], op0=op, op1=ALU.mult, accum_out=cols[:, f, j:j + 1]))
                link(v.tensor_scalar(cols[:, 1, :], cols[:, 1, :], -1.0, 1.0, ALU.mult, ALU.add))
                link(v.tensor_scalar(cols[:, 0, :], cols[:, 0, :], 1.0, None, ALU.subtract))
                link(v.scalar_tensor_tensor(out=cols[:, 2, :], in0=cols[:, 0, :], scalar=float(-NB), in1=cols[:, 2, :], op0=ALU.add, op1=ALU.mult))
                link(v.tensor_scalar(cols[:, 2, :], cols[:, 2, :], float(NB), None, ALU.add))
                if a == 1:
                    dve.wait_ge(rows_done, 1)
                for f in range(3):
                    for j in range(J):
                        dg = v.tensor_scalar(diag[:, f * J + j, :], ident[:, :], cols[:, f, j:j + 1], None, ALU.mult)
                        if (f, j) == (2, J - 1):
                            dg.then_inc(diag_done, 1)
                link(v.tensor_copy(it_i[:, :], end[:, NB - 1:NB]))
                link(v.tensor_scalar(it_i[:, :], it_i[:, :], U - 1, None, ALU.add))
                link(v.tensor_scalar(iters[a][:, :], it_i[:, :], U.bit_length() - 1, None, ALU.logical_shift_right))
                dve.wait_ge(rows_done, a + 1)
                for j in range(J):
                    v.tensor_copy(ids[a][:, 0, j * 128:(j + 1) * 128], rows[j][:, 0:128])
                    v.tensor_copy(keep[a][:, j * 128:(j + 1) * 128], rows[j][:, 128:256])
                    v.tensor_scalar(fresh[a][:, j * 128:(j + 1) * 128], rows[j][:, 128:256], -1.0, 1.0, ALU.mult, ALU.add)
                    link(v.tensor_copy(ids[a][:, 1, j * 128:(j + 1) * 128], rows[j][:, 256:384]))

            with dve.Fori(0, T // CH) as i:
                for c in range(CH):
                    tally(0, i * CH + c, i * CH + c)
            dve.wait_ge(hist[0], T + 1)
            link(v.memset(junk[0][:, :], 0.0))
            v.memset(junk[1][:, :], 0.0).then_inc(hist_done, 1)
            starts(0)
            with dve.Fori(0, T // CH) as i:
                for c in range(CH):
                    col = i * CH + c
                    rank(0, col)
                    tally(1, col, col)
                    tally(0, col, T + col)
            dve.wait_ge(hist[1], T + 1)
            link(v.memset(junk[0][:, :], 0.0))
            v.memset(junk[1][:, :], 0.0).then_inc(hist_done, 1)
            starts(1)
            with dve.Fori(0, T // CH) as i:
                for c in range(CH):
                    col = i * CH + c
                    rank(1, col)
                    tally(1, col, T + col)
            n = 0

            def nl(ins):
                nonlocal n
                n += 1
                ins.then_inc(pord, 1)
                dve.wait_ge(pord, n)

            def last(b):
                u = b % 2
                dve.wait_ge(rooted, b + 1)
                nl(v.reciprocal(pst[:, u, 3, :], pst[:, u, 2, :]))
                if b >= 2:
                    dve.wait_ge(h_out[u], 16 * (b // 2))
                v.scalar_tensor_tensor(out=ph[:, u, :, :], in0=pc_[:, u, :, :], scalar=0.0,
                                       in1=pst[:, u, 3, :].unsqueeze(2).to_broadcast([128, PC, D]), op0=ALU.max, op1=ALU.mult).then_inc(normed, 1)

            for b in range(NP):
                u = b % 2
                dve.wait_ge(x_in[u], 16 * (b // 2 + 1))
                nl(v.tensor_reduce(pst[:, u, 0, :], px[:, u, :, :], AX.X, ALU.add))
                nl(v.tensor_scalar(pst[:, u, 0, :], pst[:, u, 0, :], -1.0 / D, None, ALU.mult))
                if b >= 2:
                    dve.wait_ge(normed, b - 1)
                v.tensor_tensor(pc_[:, u, :, :], px[:, u, :, :], pst[:, u, 0, :].unsqueeze(2).to_broadcast([128, PC, D]), ALU.add).then_inc(centred, 1)
                if b >= 1:
                    last(b - 1)
                dve.wait_ge(squared, b + 1)
                v.tensor_reduce(pst[:, u, 1, :], psq[:, u, :, :], AX.X, ALU.add).then_inc(varied, 1)
            last(NP - 1)


def until(eng, sem, count):
    if not (isinstance(count, int) and count <= 0):
        eng.wait_ge(sem, count)


def phase(nc, io, keepers, tag, a, rows_of, h_of, x_of, weights, bias, x_to, h_to,
          degrees=False, weighted=False, relational=False, norm=True):
    with ExitStack() as ctx:
        sb, ps, sem = tensors(nc, ctx)
        iota, ident, eps = keepers["iota"], keepers["ident"], keepers["eps"]
        keep, fresh, ids, iters, dinv = (keepers[n][a] for n in ("keep", "fresh", "ids", "iters", "dinv"))
        sage = bias is not None
        own = weights is not None
        q = lambda name: f"{tag}_{name}"
        edges = sb(q("edges"), [128, U, K, PW])
        far = sb(q("far"), [128, U, K, D])
        apart = sb(q("apart"), [128, 2, K, 128])
        place = sb(q("place"), [128, U, K, 128])
        chunk = sb(q("chunk"), [128, U, K, C])
        spread = sb(q("spread"), [128, U, K, W])
        agg = sb(q("agg"), [128, U, W])
        deg = sb(q("deg"), [128, U, C])
        mean = sb(q("mean"), [128, U, W])
        hb, xb = sb(q("hb"), [128, U, W]), sb(q("xb"), [128, U, W])
        turned = sb(q("turned"), [128, 2, 4, 128])
        xn, xc = sb(q("xn"), [128, U, W]), sb(q("xc"), [128, U, W])
        sq, hn, st = sb(q("sq"), [128, U, W]), sb(q("hn"), [128, U, W]), sb(q("st"), [128, U, 4, C])
        ps_sum = [ps(q(f"ps_sum{k}"), [128, 512]) for k in range(2)]
        ps_turn = ps(q("ps_turn"), [128, 4, 128])
        if sage:
            ps_mix = [ps(q(f"ps_mix{k}"), [128, 512]) for k in range(2)]
        if relational:
            kind = sb(q("kind"), [128, U, K, REL])
            by_kind = sb(q("by_kind"), [128, 2, K, REL * D])
            kind_turned = sb(q("kind_turned"), [128, 2, 4, 128])
            ps_kind = [ps(q(f"ps_kind{k}"), [128, 4, 128]) for k in range(2)]
            ps_msg = [ps(q(f"ps_msg{k}"), [128, 512]) for k in range(2)]

        S = lambda name: [sem(q(f"{name}{u}")) for u in range(U)]
        edges_in, far_in, own_in, x_in, stored = S("edges_in"), S("far_in"), S("own_in"), S("x_in"), S("stored")
        placed, hot, spread_made, summed, added = S("placed"), S("hot"), S("spread_made"), S("summed"), S("added")
        meaned, product_made, mixed = S("meaned"), S("product_made"), S("mixed")
        totalled, centred, squared, varied, rooted, inverted, normed = (S(n) for n in ("totalled", "centred", "squared", "varied", "rooted", "inverted", "normed"))
        turn_made, turn_out = S("turn_made"), S("turn_out")
        distance, taken, primed = sem(q("distance")), sem(q("slot_taken")), sem(q("primed"))
        if degrees:
            counted, clamped, inverse = S("counted"), S("clamped"), S("inverse")
        if relational:
            kind_hot, kinds_made, messages = S("kind_hot"), S("kinds_made"), S("messages")
            kinds_turned, kinds_out = sem(q("kinds_turned")), sem(q("kinds_out"))
        block = ctx.enter_context(nc.Block())
        lead = LEAD if relational else LEAD - 1
        norm_lead = 2 if relational else 1
        n_out = int(x_to is not None) + int(h_to is not None)

        def view(t):
            return t.rearrange("(b p c) d -> b p (c d)", p=128, c=C)

        def cd(ap):
            return ap.rearrange("p (c d) -> p c d", d=D)

        def wide(ap):
            return ap.unsqueeze(2).to_broadcast([128, C, D])

        def steps(eng, stages):
            for n in range(-lead, U):
                for stage, ahead in stages:
                    if n + ahead >= 0:
                        stage(n + ahead, (n + ahead) % U, (n + ahead) // U)
            with eng.Fori(1, eng.value_load(iters[0:1, 0:1], min_val=1, max_val=ITERS)) as i:
                for u in range(U):
                    for stage, ahead in stages:
                        stage(i * U + (u + ahead), (u + ahead) % U, i + (u + ahead) // U)

        def land(eng, sems, per_use, ahead):
            count = eng.value_load(iters[0:1, 0:1], min_val=1, max_val=ITERS)
            for u in range(U):
                eng.wait_ge(sems[u], (count + (ahead + U - 1 - u) // U) * 16 * per_use)
                eng.sem_inc(taken, 1)

        def before(u, r, back):
            return (u - back) % U, (r + 1 if u >= back else r)

        def store(eng):
            def stage(n, u, r):
                b = eng.value_load(ids[0:1, 1, bass.ds(n, 1)], min_val=0, max_val=NB)
                until(eng, normed[u] if norm else mixed[u], r + 1)
                for t, src in ((x_to, xn), (h_to, hn)):
                    if t is not None:
                        eng.dma_start(view(io[t])[bass.ds(b, 1), :, :].rearrange("b p w -> (b p) w"), src[:, u, :]).then_inc(stored[u], 16)
            return stage

        @block.sync
        def _(sp):
            def fetch_edges(n, u, r):
                until(sp, placed[u], r)
                until(sp, spread_made[u], r)
                sp.dma_start(edges[:, u, :, :].rearrange("p k w -> p (k w)"),
                             io["tab"][a][bass.ds(n * CAP, CAP), :].rearrange("(p k) w -> p (k w)", k=K)).then_inc(edges_in[u], 16)

            def fetch_block(t, dst, arrived, used):
                def stage(n, u, r):
                    b = sp.value_load(ids[0:1, 0, bass.ds(n, 1)], min_val=0, max_val=NB - 1)
                    until(sp, used[u], r)
                    sp.dma_start(dst[:, u, :], view(io[t])[bass.ds(b, 1), :, :].rearrange("b p w -> (b p) w")).then_inc(arrived[u], 16)
                return stage

            own_ahead, x_ahead = lead if relational else 5, norm_lead + 3
            steps(sp, [(fetch_edges, lead), *([(fetch_block(h_of, hb, own_in, turn_out), own_ahead)] if own else []),
                       *([(fetch_block(x_of, xb, x_in, mixed), x_ahead)] if x_of else []),
                       *([(store(sp), 0)] if relational else [])])
            if relational:
                land(sp, stored, n_out, 0)
            land(sp, edges_in, 1, lead)
            if own:
                land(sp, own_in, 1, own_ahead)
            if x_of:
                land(sp, x_in, 1, x_ahead)

        @block.gpsimd
        def _(pool):
            def gather(n, u, r):
                until(pool, edges_in[u], r * 16 + 16)
                pool.sem_inc(taken, 1)
                until(pool, kinds_made[u] if relational else spread_made[u], r)
                pool.sem_inc(taken, 1)
                for k in range(K):
                    nc.gpsimd.indirect_dma_start(
                        out=far[:, u, k, :], out_offset=None, in_=io[rows_of][0:NB * BLK, :],
                        in_offset=bass.IndirectOffsetOnAxis(ap=edges[:, u, k, 0:1].bitcast(i32), axis=0)).then_inc(far_in[u], 16)

            steps(pool, [(gather, lead)])
            land(pool, far_in, K, lead)

        @block.tensor
        def _(pe):
            def front(n, u, r):
                until(pe, placed[u], r + 1)
                until(pe, spread_made[u], r + 1)
                v, c = before(u, r, 2)
                until(pe, added[v], c)
                p = ps_sum[u % 2]
                for k in range(K):
                    mm = nc.tensor.matmul(p[:, 0:W], place[:, u, k, :], spread[:, u, k, :], start=(k == 0), stop=(k == K - 1 and not relational))
                if relational:
                    until(pe, turn_out[u], r + 1)
                    for j in range(2):
                        mm = nc.tensor.matmul(p[:, j * 128:(j + 1) * 128], turned[:, u % 2, 2 + j, :], keepers[weights][:, 1, :],
                                              start=False, stop=False, skip_group_check=True)
                    mm = nc.tensor.matmul(p[:, 0:W], keepers["ones3"][:, :], keepers["zeros3"][:, :], start=False, stop=True)
                if degrees:
                    for k in range(K):
                        mm = nc.tensor.matmul(p[:, W:W + C], place[:, u, k, :], chunk[:, u, k, :], start=(k == 0), stop=(k == K - 1))
                mm.then_inc(summed[u], 1)

            def turn(n, u, r):
                until(pe, own_in[u], (r + 1) * 16)
                v, c = before(u, r, 1)
                until(pe, turn_out[v], c)
                if sage:
                    until(pe, meaned[u], r + 1)
                for s, t in ((0, mean), (1, hb)) if sage else ((1, hb),):
                    for j in range(2):
                        tr = nc.tensor.transpose(ps_turn[:, 2 * s + j, :], t[:, u, j * 128:(j + 1) * 128], ident[:, :])
                tr.then_inc(turn_made[u], 1)

            def product(n, u, r):
                until(pe, turn_out[u], r + 1)
                v, c = before(u, r, 2)
                until(pe, mixed[v], c)
                for j in range(2):
                    half = ps_mix[u % 2][:, j * 128:(j + 1) * 128]
                    nc.tensor.matmul(half, keepers["ones3"][:, :], keepers[bias][:, j * 128:(j + 1) * 128], start=True, stop=False)
                    for s in range(2):
                        mm = nc.tensor.matmul(half, turned[:, u % 2, 2 * s + j, :], keepers[weights][:, s, :], start=False, stop=(s == 1))
                mm.then_inc(product_made[u], 1)

            def transpose(k):
                def stage(n, u, r):
                    if k == 0:
                        until(pe, kinds_made[u], r + 1)
                    if u * K + k >= 2 or not isinstance(n, int):
                        until(pe, kinds_out, n * K + k - 1)
                    for j in range(4):
                        t = nc.tensor.transpose(ps_kind[(u * K + k) % 2][:, j, :], by_kind[:, u % 2, k, j * 128:(j + 1) * 128], ident[:, :])
                    t.then_inc(kinds_turned, 1)
                return stage

            def multiply(k):
                def stage(n, u, r):
                    if k == 0:
                        v, c = before(u, r, 2)
                        until(pe, spread_made[v], c)
                    until(pe, kinds_out, n * K + k + 1)
                    for j in range(4):
                        mm = nc.tensor.matmul(ps_msg[u % 2][:, k * D:(k + 1) * D], kind_turned[:, (u * K + k) % 2, j, :],
                                              keepers["w_rel"][:, j, :], start=(j == 0), stop=(j == 3))
                    if k == K - 1:
                        mm.then_inc(messages[u], 1)
                return stage

            if relational:
                steps(pe, [(transpose(0), 7), (transpose(1), 7), (front, 5), (multiply(0), 7), (transpose(2), 7), (multiply(1), 7),
                           (turn, 6), (multiply(2), 7)])
            elif sage:
                steps(pe, [(product, 2), (turn, 3), (front, 5)])
            else:
                steps(pe, [(front, 5)])

        @block.scalar
        def _(act):
            def distances(n, u, r):
                until(act, edges_in[u], r * 16 + 16)
                for k in range(K):
                    d = nc.scalar.activation(apart[:, u % 2, k, :], iota[:, 0:128], ACT.Abs, bias=edges[:, u, k, 1:2])
                d.then_inc(distance, 1)

            def placing(n, u, r):
                until(act, summed[u], r)
                until(act, distance, n + 1)
                nc.scalar.activation(place[:, u, :, :], apart[:, u % 2, :, :], ACT.Relu, bias=1.0, scale=-1.0).then_inc(placed[u], 1)

            def squares(n, u, r):
                until(act, centred[u], r + 1)
                until(act, varied[u], r)
                nc.scalar.activation(sq[:, u, :], xc[:, u, :], ACT.Square).then_inc(squared[u], 1)

            def root(n, u, r):
                until(act, varied[u], r + 1)
                nc.scalar.activation(st[:, u, 2, :], st[:, u, 1, :], ACT.Sqrt, bias=eps[:, :], scale=1.0 / D).then_inc(rooted[u], 1)

            def kinds(k):
                def stage(n, u, r):
                    until(act, kinds_turned, n * K + k + 1)
                    s = (u * K + k) % 2
                    nc.scalar.activation(kind_turned[:, s, :, :], ps_kind[s][:, :, :], ACT.Copy).then_inc(kinds_out, 1)
                return stage

            def evacuate(n, u, r):
                until(act, turn_made[u], r + 1)
                if sage:
                    nc.scalar.activation(turned[:, u % 2, :, :], ps_turn[:, :, :], ACT.Copy).then_inc(turn_out[u], 1)
                else:
                    v, c = before(u, r, 2)
                    until(act, summed[v], c)
                    nc.scalar.activation(turned[:, u % 2, 2:4, :], ps_turn[:, 2:4, :], ACT.Copy, scale=fresh[:, bass.ds(n, 1)]).then_inc(turn_out[u], 1)

            def activate(n, u, r):
                until(act, product_made[u], r + 1)
                until(act, stored[u], r * 16 * n_out)
                nc.scalar.activation(hn[:, u, :], ps_mix[u % 2][:, 0:W], ACT.Relu).then_inc(mixed[u], 1)

            place_edge = [(distances, 6), (placing, 6)]
            if relational:
                steps(act, [(kinds(0), 7), (squares, 2), (kinds(1), 7), (root, 1), (distances, 6), (kinds(2), 7), (evacuate, 6), (placing, 6)])
            elif norm:
                steps(act, [(root, 0), (distances, 6), (squares, 1), (placing, 6), *([(evacuate, 3)] if sage else []), (store(act), 0)])
            elif sage:
                steps(act, [(activate, 1), *place_edge, (evacuate, 3), (store(act), 0)])
            else:
                steps(act, [*place_edge, (store(act), 0)])
            if not relational:
                land(act, stored, n_out, 0)

        @block.vector
        def _(dve):
            v = nc.vector

            def chunks(n, u, r):
                until(dve, edges_in[u], r * 16 + 16)
                until(dve, summed[u], r)
                v.tensor_tensor(chunk[:, u, :, :], edges[:, u, :, 2:3].to_broadcast([128, K, C]),
                                iota[:, 0:C].unsqueeze(1).to_broadcast([128, K, C]), ALU.is_equal).then_inc(hot[u], 1)

            def weigh(n, u, r):
                until(dve, hot[u], 2 * r + 1)
                v.tensor_tensor(chunk[:, u, :, :], chunk[:, u, :, :], edges[:, u, :, 4:5].to_broadcast([128, K, C]), ALU.mult).then_inc(hot[u], 1)

            def spreading(k):
                def stage(n, u, r):
                    if k == 0:
                        until(dve, hot[u], (2 if weighted else 1) * (r + 1))
                        if relational:
                            until(dve, messages[u], r + 1)
                        else:
                            until(dve, far_in[u], (r + 1) * 16 * K)
                    rows = ps_msg[u % 2][:, k * D:(k + 1) * D] if relational else far[:, u, k, :]
                    s = v.tensor_tensor(cd(spread[:, u, k, :]), rows.unsqueeze(1).to_broadcast([128, C, D]), wide(chunk[:, u, k, :]), ALU.mult)
                    if k == K - 1:
                        s.then_inc(spread_made[u], 1)
                return stage

            def kinds_hot(n, u, r):
                until(dve, edges_in[u], r * 16 + 16)
                v.tensor_tensor(kind[:, u, :, :], edges[:, u, :, 3:4].to_broadcast([128, K, REL]),
                                iota[:, 0:REL].unsqueeze(1).to_broadcast([128, K, REL]), ALU.is_equal).then_inc(kind_hot[u], 1)

            def kinds(k):
                def stage(n, u, r):
                    if k == 0:
                        until(dve, kind_hot[u], r + 1)
                        until(dve, far_in[u], (r + 1) * 16 * K)
                        w, c = before(u, r, 2)
                        until(dve, messages[w], c)
                    s = v.tensor_tensor(by_kind[:, u % 2, k, :].rearrange("p (r d) -> p r d", d=D), far[:, u, k, :].unsqueeze(1).to_broadcast([128, REL, D]),
                                        kind[:, u, k, :].unsqueeze(2).to_broadcast([128, REL, D]), ALU.mult)
                    if k == K - 1:
                        s.then_inc(kinds_made[u], 1)
                return stage

            def count(n, u, r):
                until(dve, summed[u], r + 1)
                w, c = before(u, r, 1)
                until(dve, counted[w], c)
                v.scalar_tensor_tensor(out=deg[:, u, :], in0=deg[:, (u - 1) % U, :], scalar=keep[:, bass.ds(n, 1)],
                                       in1=ps_sum[u % 2][:, W:W + C], op0=ALU.mult, op1=ALU.add).then_inc(counted[u], 1)

            def add_up(n, u, r):
                until(dve, summed[u], r + 1)
                w, c = before(u, r, 1)
                until(dve, added[w], c)
                v.scalar_tensor_tensor(out=agg[:, u, :], in0=agg[:, (u - 1) % U, :], scalar=keep[:, bass.ds(n, 1)],
                                       in1=ps_sum[u % 2][:, 0:W], op0=ALU.mult, op1=ALU.add).then_inc(added[u], 1)

            def clamp(n, u, r):
                until(dve, counted[u], r + 1)
                v.tensor_scalar(st[:, u, 3, :], deg[:, u, :], 1.0, None, ALU.max).then_inc(clamped[u], 1)

            def invert(n, u, r):
                until(dve, clamped[u], r + 1)
                v.reciprocal(dinv[:, bass.ds(n, 1), :], st[:, u, 3, :].unsqueeze(1)).then_inc(inverse[u], 1)

            def average(n, u, r):
                if degrees:
                    until(dve, inverse[u], r + 1)
                until(dve, added[u], r + 1)
                v.tensor_tensor(cd(mean[:, u, :]), cd(agg[:, u, :]), wide(dinv[:, bass.ds(n, 1), :].rearrange("p a c -> p (a c)")), ALU.mult).then_inc(meaned[u], 1)

            def mix(n, u, r):
                until(dve, x_in[u], (r + 1) * 16)
                until(dve, stored[u], r * 16 * n_out)
                if sage:
                    until(dve, product_made[u], r + 1)
                else:
                    until(dve, added[u], r + 1)
                if own:
                    v.scalar_tensor_tensor(out=xn[:, u, :], in0=ps_mix[u % 2][:, 0:W] if sage else agg[:, u, :], scalar=0.0, in1=xb[:, u, :],
                                           op0=ALU.max, op1=ALU.add).then_inc(mixed[u], 1)
                else:
                    v.tensor_tensor(xn[:, u, :], agg[:, u, :], xb[:, u, :], ALU.add).then_inc(mixed[u], 1)

            def total(n, u, r):
                until(dve, mixed[u], r + 1)
                v.tensor_reduce(st[:, u, 0, :], cd(xn[:, u, :]), AX.X, ALU.add, negate=True).then_inc(totalled[u], 1)

            def centre(n, u, r):
                until(dve, totalled[u], r + 1)
                v.scalar_tensor_tensor(out=cd(xc[:, u, :]), in0=wide(st[:, u, 0, :]), scalar=1.0 / D, in1=cd(xn[:, u, :]),
                                       op0=ALU.mult, op1=ALU.add).then_inc(centred[u], 1)

            def variance(n, u, r):
                until(dve, squared[u], r + 1)
                v.tensor_reduce(st[:, u, 1, :], cd(sq[:, u, :]), AX.X, ALU.add).then_inc(varied[u], 1)

            def reciprocal(n, u, r):
                until(dve, rooted[u], r + 1)
                v.reciprocal(st[:, u, 3, :], st[:, u, 2, :]).then_inc(inverted[u], 1)

            def last(n, u, r):
                until(dve, inverted[u], r + 1)
                v.scalar_tensor_tensor(out=cd(hn[:, u, :]), in0=cd(xc[:, u, :]), scalar=0.0, in1=wide(st[:, u, 3, :]),
                                       op0=ALU.max, op1=ALU.mult).then_inc(normed[u], 1)

            v.memset(agg[:, U - 1, :], 0.0).then_inc(primed, 1)
            v.memset(deg[:, U - 1, :], 0.0).then_inc(primed, 1)
            until(dve, primed, 2)
            s0, s1, s2 = ((spreading(k), 5) for k in range(K))
            if degrees:
                steps(dve, [(chunks, 5), (count, 3), (add_up, 3), (clamp, 3), s0, (invert, 3), s1, (average, 3), s2])
            elif relational:
                steps(dve, [(kinds_hot, 7), (mix, 2), (chunks, 5), (total, 2), (variance, 1), (centre, 2), (add_up, 3),
                            (kinds(0), 7), (reciprocal, 0), (kinds(1), 7), (kinds(2), 7), s0, (last, 0), s1, s2])
            elif norm:
                steps(dve, [(mix, 1), (chunks, 5), (total, 1), (variance, 0), (centre, 1), (add_up, 3), s0, (reciprocal, 0),
                            *([(average, 3)] if sage else []), s1, (last, 0), s2])
            else:
                steps(dve, [(chunks, 5), (mix, 1), *([(weigh, 5)] if weighted else []), (add_up, 3), s0, s1, s2])


def load_weights(nc, io, keepers):
    with ExitStack() as ctx:
        sb, _, sem = tensors(nc, ctx)
        cleared, loaded, parts, moved, order = (sem(n) for n in ("weights_cleared", "weights_loaded", "bias_parts", "parts_moved", "bias_order"))
        bias, part, rest = sb("bias_row", [1, 2, W]), sb("bias_part", [1, 2, 3, W], bf16), sb("bias_rest", [1, 2, W])
        pairs = (("w_sage0", "sage0"), ("w_sage1", "sage1"), ("w_self", "own"))
        block = ctx.enter_context(nc.Block())

        @block.gpsimd
        def _(pool):
            for _, dst in pairs:
                nc.gpsimd.memset(keepers[dst][:, :, :], 0.0).then_inc(cleared, 1)

        @block.sync
        def _(sp):
            sp.dma_start(bias[:, 0, :], io["b0"].unsqueeze(0)).then_inc(loaded, 16)
            sp.dma_start(bias[:, 1, :], io["b1"].unsqueeze(0)).then_inc(loaded, 16)
            sp.wait_ge(loaded, 32)
            sp.wait_ge(cleared, len(pairs))
            for name, dst in pairs:
                for half in range(2):
                    own = slice(D * half, D * half + D)
                    sp.dma_start(keepers[dst][own, :, own], io[name].rearrange("s i o -> i s o")).then_inc(loaded, 16)
            for j in range(REL // 2):
                for half in range(2):
                    sp.dma_start(keepers["w_rel"][D * half:D * half + D, j, :], io["w_rel"][2 * j + half, :, :]).then_inc(loaded, 16)
            sp.wait_ge(parts, 2)
            for b in range(2):
                for k in range(3):
                    sp.dma_start(keepers[f"b{b}"][k:k + 1, :], part[:, b, k, :]).then_inc(moved, 16)
            sp.wait_ge(loaded, 16 * (2 + 2 * len(pairs) + REL))
            sp.wait_ge(moved, 16 * 6)

        @block.vector
        def _(dve):
            v = nc.vector
            v.memset(keepers["zeros3"][:, :], 0.0)
            v.memset(keepers["ones3"][:, :], 1.0).then_inc(parts, 1)
            dve.wait_ge(loaded, 32)
            v.tensor_copy(part[:, :, 0, :], bias[:, :, :]).then_inc(order, 1)
            dve.wait_ge(order, 1)
            v.tensor_tensor(rest[:, :, :], bias[:, :, :], part[:, :, 0, :], ALU.subtract).then_inc(order, 1)
            dve.wait_ge(order, 2)
            v.tensor_copy(part[:, :, 1, :], rest[:, :, :]).then_inc(order, 1)
            dve.wait_ge(order, 3)
            v.tensor_tensor(rest[:, :, :], rest[:, :, :], part[:, :, 1, :], ALU.subtract).then_inc(order, 1)
            dve.wait_ge(order, 4)
            v.tensor_copy(part[:, :, 2, :], rest[:, :, :]).then_inc(parts, 1)


def build(nc, io):
    with ExitStack() as ctx:
        def sb(name, shape, dt=fp32):
            return ctx.enter_context(nc.sbuf_tensor(name, shape, dt))

        for name in ("H0", "H1", "X1", "H3", "X2", "H4", "X3", "H5"):
            io[name] = nc.dram_tensor(name, (NROWS, D), fp32).ap()
        io["tab"] = [nc.dram_tensor(f"placed_{a}", (TROWS, PW), fp32).ap() for a in ("dst", "src")]
        keepers = {
            "iota": sb("iota", [128, NB + 1]), "ident": sb("ident", [128, 128]), "eps": sb("eps", [128, 1]),
            "keep": [sb(f"keep{a}", [128, J * 128]) for a in range(2)],
            "fresh": [sb(f"fresh{a}", [128, J * 128]) for a in range(2)],
            "ids": [sb(f"ids{a}", [128, 2, J * 128], i32) for a in range(2)],
            "iters": [sb(f"iters{a}", [128, 1], i32) for a in range(2)],
            "dinv": [sb("dinv", [128, J * 128, C])] * 2,
            "sage0": sb("w_sage0", [128, 2, 2 * D]), "sage1": sb("w_sage1", [128, 2, 2 * D]), "own": sb("w_own", [128, 2, 2 * D]),
            "w_rel": sb("w_rel", [128, REL // 2, D]), "ones3": sb("ones3", [3, 128], bf16), "zeros3": sb("zeros3", [3, W], bf16),
            "b0": sb("b0", [3, W], bf16), "b1": sb("b1", [3, W], bf16),
        }
        load_weights(nc, io, keepers)
        place_edges(nc, io, keepers)
        phase(nc, io, keepers, "A", 0, "H0", "H0", None, "sage0", "b0", None, "H1", degrees=True, norm=False)
        phase(nc, io, keepers, "B", 0, "H1", "H1", "x", "sage1", "b1", "X1", "H3")
        phase(nc, io, keepers, "C", 1, "H3", None, "X1", None, None, "X2", "H4")
        phase(nc, io, keepers, "D", 0, "H4", "H4", "X2", "own", None, "X3", "H5", relational=True)
        phase(nc, io, keepers, "E", 0, "H5", None, "X3", None, None, "out", None, weighted=True, norm=False)


def kernel(**inputs):
    import numpy as np
    import concourse.bacc as bacc
    from concourse.bass_utils import run_bass_kernel_spmd as run

    def padded(a, n, fill):
        out = np.full((n, *a.shape[1:]), fill, a.dtype)
        out[:len(a)] = a
        return out

    g = {k: np.asarray(v) for k, v in inputs.items()}
    arrays = {
        "x": padded(g["x"], NROWS, 0),
        "dst": padded(g["dst"].astype(np.int32), 128 * T, NB * BLK),
        "src": padded(g["src"].astype(np.int32), 128 * T, NB * BLK),
        "etype": padded(g["edge_type_8"].astype(np.int32), 128 * T, 0),
        "ew": padded(g["edge_weight"], 128 * T, 0),
        "w_sage0": np.stack([g["L0_gnn_W_neigh0"], g["L0_gnn_W_self0"]]),
        "w_sage1": np.stack([g["L0_gnn_W_neigh1"], g["L0_gnn_W_self1"]]),
        "w_self": np.ascontiguousarray(np.stack([g["L2_gnn_self_loop_w"].T, g["L2_gnn_self_loop_w"].T])),
        "w_rel": g["L2_gnn_weight"], 
        "b0": np.tile(g["L0_gnn_b0"], C), "b1": np.tile(g["L0_gnn_b1"], C),
    }
    nc = bacc.Bacc("TRN2", target_bir_lowering=False, num_devices=1)
    io = {n: nc.dram_tensor(f"in_{n}", a.shape, i32 if a.dtype == np.int32 else fp32, kind="ExternalInput").ap() for n, a in arrays.items()}
    io["out"] = nc.dram_tensor("out_x", (NROWS, D), fp32, kind="ExternalOutput").ap()
    build(nc, io)
    r = run(nc, [{f"in_{n}": np.ascontiguousarray(a) for n, a in arrays.items()}], core_ids=[0])
    return r.results[0]["out_x"][:N]
```

```python
import concourse.bass as bass
import numpy as np
from concourse import mybir
from contextlib import ExitStack

N, D, E, REL = 100000, 64, 50000, 8
C, K, U = 4, 3, 4
BLK, CAP, W = 128 * C, 128 * K, C * D
NB = -(-N // BLK)
NROWS = (NB + 1) * BLK
LEAD = 8
SMAX = NB + E // CAP
ITERS = -(-SMAX // U)
SROOM = ITERS * U + -(-LEAD // U) * U
J = -(-SROOM // 128)
PW = 5
TRASH = SROOM * CAP
TROWS = TRASH + 256
PC = 16
NP = NB * BLK // (128 * PC)
T = -(-E // (128 * NP)) * NP
CH = 14
TALLIES = [T, 0]
EPS = 1e-5
ROUND = float(3 << 22)
fp32, i32, bf16 = mybir.dt.float32, mybir.dt.int32, mybir.dt.bfloat16
ALU, ACT, AX = mybir.AluOpType, mybir.ActivationFunctionType, mybir.AxisListType
assert T % CH == 0 and TROWS * PW % 128 == 0 and NB * BLK % (128 * PC) == 0 and 128 * T - E <= 256 and NB + 1 >= 128


def tensors(nc, ctx):
    def sb(name, shape, dt=fp32):
        return ctx.enter_context(nc.sbuf_tensor(name, shape, dt))

    def ps(name, shape):
        return ctx.enter_context(nc.psum_tensor(name, shape, fp32))

    sems = []

    def clear():
        nc.clear_and_free_semaphores(sems)
        nc.all_engine_barrier()

    ctx.callback(clear)

    def sem(name):
        sems.append(nc.alloc_semaphore(name))
        return sems[-1]

    return sb, ps, sem


def place_edges(nc, io, keepers):
    with ExitStack() as ctx:
        sb, ps, sem = tensors(nc, ctx)
        iota, ident, eps = keepers["iota"], keepers["ident"], keepers["eps"]
        keep, fresh, ids, iters = keepers["keep"], keepers["fresh"], keepers["ids"], keepers["iters"]
        iota_i = sb("iota_i", [128, NB + 1], i32)
        pidx_i = sb("pidx_i", [128, J], i32)
        pidx = sb("pidx", [128, J])
        tri, ones = sb("tri", [128, 128]), sb("ones", [128, NB + 1])
        raw = [sb("dst_raw", [128, T], i32), sb("src_raw", [128, T], i32)]
        typ, wgt = sb("typ", [128, T], i32), sb("wgt", [128, T])
        tmp_i = sb("tmp_i", [128, 3, T], i32)
        blk = [sb(f"blk{a}", [128, T]) for a in range(2)]
        load = [sb(f"load{a}", [128, T, PW]) for a in range(2)]
        cur = [sb(f"cur{a}", [128, NB + 1]) for a in range(2)]
        pos = [sb(f"pos{a}", [128, T]) for a in range(2)]
        junk = [sb(f"junk{a}", [128, NB + 1]) for a in range(2)]
        nst, start = sb("nst", [128, NB]), sb("start", [128, NB])
        scan = [sb(f"scan{k}", [128, NB]) for k in range(2)]
        cols = sb("cols", [128, 3, J])
        diag = sb("diag", [128, 3 * J, 128])
        minus_blk, away = sb("minus_blk", [128, T]), sb("away", [128, CH, NB + 1])
        found, partial = sb("found", [128, CH, NB + 1]), sb("partial", [128, CH // 2, NB + 1])
        it_i = sb("it_i", [128, 1], i32)
        nothing = sb("nothing", [128, TROWS * PW // 128])
        ring_load = sb("ring_load", [128, 2, CH, PW])
        ring_pos = sb("ring_pos", [128, 2, CH], i32)
        x0, x0_centred, x0_squares, h0 = (sb(n, [128, PC, D]) for n in ("x0", "x0_centred", "x0_squares", "h0"))
        mean0, var0, root0, inverse0 = (sb(n, [128, PC]) for n in ("mean0", "var0", "root0", "inverse0"))
        after = sb("after", [128, J])
        tot = [ps(f"tot{a}", [128, 512]) for a in range(2)]
        rows = [ps(f"rows{k}", [128, 512]) for k in range(J)]

        iota_made, loaded, filled = sem("iota_made"), sem("edges_loaded"), sem("tables_filled")
        fill_made, order = sem("fill_made"), sem("vector_order")
        hist, blocks_made = [sem(f"hist{a}") for a in range(2)], sem("blocks_made")
        away_made, found_made, summed = sem("away_made"), sem("found_made"), sem("partial_sums")
        tot_done, diag_done, rows_done = sem("tot_done"), sem("diag_done"), sem("rows_done")
        ranked = [sem(f"ranked{a}") for a in range(2)]
        ring_made, ring_sent = [sem(f"ring_made{k}") for k in range(2)], [sem(f"ring_sent{k}") for k in range(2)]
        slot_taken = sem("slot_taken")
        x_in, h_out = sem("x_in"), sem("h_out")
        totalled, averaged, centred, squared, varied, rooted, inverted, normed = (
            sem(n) for n in ("totalled", "averaged", "centred", "squared", "varied", "rooted", "inverted", "normed"))
        block = ctx.enter_context(nc.Block())
        x_v = io["x"][0:NP * PC * 128, :].rearrange("(b p c) d -> b p (c d)", p=128, c=PC)
        h_v = io["H0"][0:NP * PC * 128, :].rearrange("(b p c) d -> b p (c d)", p=128, c=PC)

        @block.sync
        def _(sp):
            for raw_t, name in zip((*raw, typ, wgt), ("dst", "src", "etype", "ew")):
                sp.dma_start(raw_t[:, :], io[name].rearrange("(p t) -> p t", t=T)).then_inc(loaded, 16)
            sp.wait_ge(fill_made, 2)
            for a in range(2):
                sp.dma_start(io["tab"][a].rearrange("(p r) w -> p (r w)", p=128), nothing[:, :]).then_inc(filled, 16)

            def load_x(b):
                until(sp, centred, b)
                sp.dma_start(x0[:, :, :].rearrange("p c d -> p (c d)"), x_v[bass.ds(b, 1), :, :].rearrange("b p w -> (b p) w")).then_inc(x_in, 16)

            load_x(0)
            with sp.Fori(1, NP) as b:
                load_x(b)

        @block.gpsimd
        def _(pool):
            nc.gpsimd.iota(iota_i[:, :], pattern=[[1, NB + 1]], base=0, channel_multiplier=0).then_inc(iota_made, 1)
            nc.gpsimd.iota(pidx_i[:, :], pattern=[[128, J]], base=0, channel_multiplier=1).then_inc(iota_made, 1)
            nc.gpsimd.memset(nothing[:, :], 0.0).then_inc(fill_made, 1)
            pool.wait_ge(fill_made, 1)
            nc.gpsimd.memset(nothing[:, :].rearrange("p (r w) -> p r w", w=PW)[:, :, 1:2], 1.0).then_inc(fill_made, 1)

            nc.gpsimd.memset(partial[:, :, :], 0.0).then_inc(summed, 1)
            with pool.Fori(0, T // CH) as i:
                pool.wait_ge(found_made, i + 1)
                pool.sem_inc(slot_taken, 1)
                for half in range(2):
                    pool.wait_ge(summed, 2 * i + half + 1)
                    pool.sem_inc(slot_taken, 1)
                    nc.gpsimd.tensor_tensor(partial[:, :, :], partial[:, :, :], found[:, half * (CH // 2):(half + 1) * (CH // 2), :], ALU.add).then_inc(summed, 1)
            pool.wait_ge(filled, 32)

            def scatter(i):
                for a in range(2):
                    pool.wait_ge(ranked[a], (i + 1) * CH)
                    pool.sem_inc(slot_taken, 1)
                    until(pool, ring_sent[a], i * 16 * CH)
                    nc.gpsimd.tensor_copy(ring_load[:, a, :, :].bitcast(i32),
                                          load[a][:, bass.ds(i * CH, CH), :].bitcast(i32)).then_inc(ring_made[a], 1)
                    nc.gpsimd.tensor_copy(ring_pos[:, a, :], pos[a][:, bass.ds(i * CH, CH)]).then_inc(ring_made[a], 1)
                    pool.wait_ge(ring_made[a], i * 2 + 2)
                    pool.sem_inc(slot_taken, 1)
                    for c in range(CH):
                        nc.gpsimd.indirect_dma_start(
                            out=io["tab"][a], out_offset=bass.IndirectOffsetOnAxis(ap=ring_pos[:, a, c:c + 1], axis=0),
                            in_=ring_load[:, a, c, :], in_offset=None).then_inc(ring_sent[a], 16)

            scatter(0)
            with pool.Fori(1, T // CH) as i:
                scatter(i)
            for a in range(2):
                pool.wait_ge(ring_sent[a], T * 16)

        @block.tensor
        def _(pe):
            for a in range(2):
                pe.wait_ge(hist[a], 1 + TALLIES[a])
                nc.tensor.matmul(tot[a][:, 0:NB + 1], ones[:, 0:128], cur[a][:, :], start=True, stop=True)
                nc.tensor.matmul(tot[a][:, 256:256 + NB + 1], tri[:, :], cur[a][:, :], start=True, stop=True).then_inc(tot_done, 1)
                pe.wait_ge(diag_done, a + 1)
                for f in range(3):
                    for j in range(J):
                        mm = nc.tensor.matmul(rows[j][:, f * 128:(f + 1) * 128], ones[:, 0:128], diag[:, f * J + j, :], start=True, stop=True)
                mm.then_inc(rows_done, 1)

        @block.scalar
        def _(act):
            def find(i):
                until(act, found_made, i)
                for c in range(CH):
                    d = nc.scalar.activation(away[:, c, :], iota[:, :], ACT.Abs, bias=minus_blk[:, bass.ds(i * CH + c, 1)])
                d.then_inc(away_made, 1)
                act.wait_ge(away_made, i + 1)
                act.wait_ge(summed, 2 * i + 1)
                nc.scalar.activation(found[:, :, :], away[:, :, :], ACT.Relu, bias=1.0, scale=-1.0).then_inc(found_made, 1)

            act.wait_ge(blocks_made, 1)
            find(0)
            with act.Fori(1, T // CH) as i:
                find(i)

            def norm(b):
                act.wait_ge(centred, b + 1)
                nc.scalar.activation(x0_squares[:, :, :], x0_centred[:, :, :], ACT.Square).then_inc(squared, 1)
                act.wait_ge(varied, b + 1)
                nc.scalar.activation(root0[:, :], var0[:, :], ACT.Sqrt, bias=eps[:, :], scale=1.0 / D).then_inc(rooted, 1)
                act.wait_ge(normed, b + 1)
                act.dma_start(h_v[bass.ds(b, 1), :, :].rearrange("b p w -> (b p) w"), h0[:, :, :].rearrange("p c d -> p (c d)")).then_inc(h_out, 16)

            with act.Fori(0, NP) as b:
                norm(b)
            act.wait_ge(h_out, 16 * NP)

        @block.vector
        def _(dve):
            count = [0]

            def link(ins):
                count[0] += 1
                ins.then_inc(order, 1)
                dve.wait_ge(order, count[0])

            v = nc.vector
            v.memset(ones[:, :], 1.0)
            v.memset(eps[:, :], EPS)
            v.memset(cur[0][:, :], 0.0).then_inc(hist[0], 1)
            dve.wait_ge(iota_made, 2)
            v.tensor_copy(iota[:, :], iota_i[:, :])
            link(v.tensor_copy(pidx[:, :], pidx_i[:, :]))
            v.tensor_scalar(tri[:, :], iota[:, 0:128], pidx[:, 0:1], None, ALU.is_gt)
            v.tensor_scalar(ident[:, :], iota[:, 0:128], pidx[:, 0:1], None, ALU.is_equal)
            dve.wait_ge(loaded, 64)
            for a in range(2):
                v.tensor_scalar(tmp_i[:, 0, :], raw[a][:, :], BLK.bit_length() - 1, None, ALU.logical_shift_right)
                v.tensor_scalar(tmp_i[:, 1, :], raw[a][:, :], C.bit_length() - 1, 127, ALU.logical_shift_right, ALU.bitwise_and)
                link(v.tensor_scalar(tmp_i[:, 2, :], raw[a][:, :], C - 1, None, ALU.bitwise_and))
                v.tensor_copy(blk[a][:, :], tmp_i[:, 0, :])
                v.tensor_copy(load[a][:, :, 0].bitcast(i32), raw[1 - a][:, :])
                v.tensor_scalar(load[a][:, :, 1], tmp_i[:, 1, :], -1.0, None, ALU.mult)
                v.tensor_copy(load[a][:, :, 2], tmp_i[:, 2, :])
                v.tensor_copy(load[a][:, :, 3], typ[:, :])
                link(v.tensor_copy(load[a][:, :, 4], wgt[:, :]))
            v.tensor_scalar(after[:, :], pidx[:, :], 1.0, None, ALU.add)
            v.tensor_scalar(minus_blk[:, :], blk[1][:, :], -1.0, None, ALU.mult).then_inc(blocks_made, 1)

            def tally(a, col, seen):
                dve.wait_ge(hist[a], seen + 1)
                v.scalar_tensor_tensor(out=cur[a][:, :], in0=iota[:, :], scalar=blk[a][:, bass.ds(col, 1)], in1=cur[a][:, :],
                                       op0=ALU.is_equal, op1=ALU.add).then_inc(hist[a], 1)

            def rank(a, col):
                dve.wait_ge(hist[a], TALLIES[a] + 1 + col)
                v.scalar_tensor_tensor(out=junk[a][:, :], in0=iota[:, :], scalar=blk[a][:, bass.ds(col, 1)], in1=cur[a][:, :],
                                       op0=ALU.is_equal, op1=ALU.mult, accum_out=pos[a][:, bass.ds(col, 1)]).then_inc(ranked[a], 1)

            def starts(a):
                dve.wait_ge(tot_done, a + 1)
                link(v.tensor_scalar(nst[:, :], tot[a][:, 0:NB], 1.0 / CAP, 0.5 - 0.5 / CAP, ALU.mult, ALU.add))
                link(v.tensor_scalar(nst[:, :], nst[:, :], ROUND, ROUND, ALU.add, ALU.subtract))
                link(v.tensor_scalar(nst[:, :], nst[:, :], 1.0, None, ALU.max))
                link(v.tensor_copy(scan[0][:, :], nst[:, :]))
                s, k = 1, 0
                while s < NB:
                    v.tensor_copy(scan[1 - k][:, 0:s], scan[k][:, 0:s])
                    link(v.tensor_tensor(scan[1 - k][:, s:NB], scan[k][:, s:NB], scan[k][:, 0:NB - s], ALU.add))
                    s, k = 2 * s, 1 - k
                end = scan[k]
                link(v.tensor_tensor(start[:, :], end[:, :], nst[:, :], ALU.subtract))
                link(v.tensor_scalar(cur[a][:, 0:NB], start[:, :], float(CAP), None, ALU.mult))
                v.tensor_tensor(cur[a][:, 0:NB], cur[a][:, 0:NB], tot[a][:, 256:256 + NB], ALU.add)
                v.tensor_scalar(cur[a][:, NB:NB + 1], tot[a][:, 256 + NB:257 + NB], float(TRASH), None, ALU.add)
                for j in range(J):
                    for f, (row, op) in enumerate(((start, ALU.is_le), (start, ALU.is_equal), (end, ALU.is_equal))):
                        link(v.scalar_tensor_tensor(out=junk[0][:, 0:NB], in0=row[:, :], scalar=(after if f == 2 else pidx)[:, j:j + 1],
                                                    in1=ones[:, 0:NB], op0=op, op1=ALU.mult, accum_out=cols[:, f, j:j + 1]))
                link(v.tensor_scalar(cols[:, 1, :], cols[:, 1, :], -1.0, 1.0, ALU.mult, ALU.add))
                link(v.tensor_scalar(cols[:, 0, :], cols[:, 0, :], 1.0, None, ALU.subtract))
                link(v.scalar_tensor_tensor(out=cols[:, 2, :], in0=cols[:, 0, :], scalar=float(-NB), in1=cols[:, 2, :], op0=ALU.add, op1=ALU.mult))
                link(v.tensor_scalar(cols[:, 2, :], cols[:, 2, :], float(NB), None, ALU.add))
                if a == 1:
                    dve.wait_ge(rows_done, 1)
                for f in range(3):
                    for j in range(J):
                        dg = v.tensor_scalar(diag[:, f * J + j, :], ident[:, :], cols[:, f, j:j + 1], None, ALU.mult)
                        if (f, j) == (2, J - 1):
                            dg.then_inc(diag_done, 1)
                link(v.tensor_copy(it_i[:, :], end[:, NB - 1:NB]))
                link(v.tensor_scalar(it_i[:, :], it_i[:, :], U - 1, None, ALU.add))
                link(v.tensor_scalar(iters[a][:, :], it_i[:, :], U.bit_length() - 1, None, ALU.logical_shift_right))
                dve.wait_ge(rows_done, a + 1)
                for j in range(J):
                    v.tensor_copy(ids[a][:, 0, j * 128:(j + 1) * 128], rows[j][:, 0:128])
                    v.tensor_copy(keep[a][:, j * 128:(j + 1) * 128], rows[j][:, 128:256])
                    v.tensor_scalar(fresh[a][:, j * 128:(j + 1) * 128], rows[j][:, 128:256], -1.0, 1.0, ALU.mult, ALU.add)
                    link(v.tensor_copy(ids[a][:, 1, j * 128:(j + 1) * 128], rows[j][:, 256:384]))

            with dve.Fori(0, T // CH) as i:
                for c in range(CH):
                    tally(0, i * CH + c, i * CH + c)
            starts(0)
            dve.wait_ge(summed, 1 + 2 * (T // CH))
            v.tensor_reduce(cur[1][:, :], partial[:, :, :].rearrange("p c n -> p n c"), AX.X, ALU.add).then_inc(hist[1], 1)
            starts(1)

            def total(b):
                dve.wait_ge(x_in, 16 * b + 16)
                v.tensor_reduce(mean0[:, :], x0[:, :, :], AX.X, ALU.add, negate=True).then_inc(totalled, 1)

            def average(b):
                dve.wait_ge(totalled, b + 1)
                v.tensor_scalar(mean0[:, :], mean0[:, :], 1.0 / D, None, ALU.mult).then_inc(averaged, 1)

            def centre(b):
                dve.wait_ge(averaged, b + 1)
                v.tensor_tensor(x0_centred[:, :, :], x0[:, :, :], mean0[:, :].unsqueeze(2).to_broadcast([128, PC, D]), ALU.add).then_inc(centred, 1)

            def variance(b):
                dve.wait_ge(squared, b + 1)
                v.tensor_reduce(var0[:, :], x0_squares[:, :, :], AX.X, ALU.add).then_inc(varied, 1)

            def invert(b):
                dve.wait_ge(rooted, b + 1)
                v.reciprocal(inverse0[:, :], root0[:, :]).then_inc(inverted, 1)

            def last(b):
                dve.wait_ge(inverted, b + 1)
                until(dve, h_out, 16 * b)
                v.scalar_tensor_tensor(out=h0[:, :, :], in0=x0_centred[:, :, :], scalar=0.0,
                                       in1=inverse0[:, :].unsqueeze(2).to_broadcast([128, PC, D]), op0=ALU.max, op1=ALU.mult).then_inc(normed, 1)

            norm_at = {0: total, 1: average, 2: centre, 4: variance, 6: invert, 7: last}

            def ranks(b):
                for c in range(T // NP):
                    col = b * (T // NP) + c
                    rank(0, col)
                    rank(1, col)
                    tally(0, col, TALLIES[0] + col)
                    tally(1, col, TALLIES[1] + col)
                    if c in norm_at:
                        norm_at[c](b)

            ranks(0)
            with dve.Fori(1, NP) as b:
                ranks(b)


def until(eng, sem, count):
    if not (isinstance(count, int) and count <= 0):
        eng.wait_ge(sem, count)


def phase(nc, io, keepers, tag, a, rows_of, h_of, x_of, weights, bias, x_to, h_to,
          degrees=False, weighted=False, relational=False, norm=True):
    with ExitStack() as ctx:
        sb, ps, sem = tensors(nc, ctx)
        iota, ident, eps = keepers["iota"], keepers["ident"], keepers["eps"]
        keep, fresh, ids, iters, dinv = (keepers[n][a] for n in ("keep", "fresh", "ids", "iters", "dinv"))
        sage = bias is not None
        own = weights is not None
        q = lambda name: f"{tag}_{name}"
        edges = sb(q("edges"), [128, U, K, PW])
        far = sb(q("far"), [128, U, K, D])
        apart = sb(q("apart"), [128, 2, K, 128])
        place = sb(q("place"), [128, U, K, 128])
        spread = sb(q("spread"), [128, U, K, W + C])
        agg = sb(q("agg"), [128, U, W])
        deg = sb(q("deg"), [128, U, C])
        mean = sb(q("mean"), [128, U, W])
        hb, xb = sb(q("hb"), [128, U, W]), sb(q("xb"), [128, U, W])
        turned = sb(q("turned"), [128, 2, 4, 128])
        xn, xc = sb(q("xn"), [128, U, W]), sb(q("xc"), [128, U, W])
        sq, hn, st = sb(q("sq"), [128, U, W]), sb(q("hn"), [128, U, W]), sb(q("st"), [128, U, 4, C])
        ps_sum = [ps(q(f"ps_sum{k}"), [128, 512]) for k in range(2)]
        ps_turn = ps(q("ps_turn"), [128, 4, 128])
        if sage:
            ps_mix = [ps(q(f"ps_mix{k}"), [128, 512]) for k in range(2)]
        if relational:
            kind = sb(q("kind"), [128, U, K, REL])
            by_kind = sb(q("by_kind"), [128, 2, K, REL * D])
            kind_turned = sb(q("kind_turned"), [128, 2, 4, 128])
            ps_kind = [ps(q(f"ps_kind{k}"), [128, 4, 128]) for k in range(2)]
            ps_msg = [ps(q(f"ps_msg{k}"), [128, 512]) for k in range(2)]

        S = lambda name: [sem(q(f"{name}{u}")) for u in range(U)]
        edges_in, far_in, own_in, x_in, stored = S("edges_in"), S("far_in"), S("own_in"), S("x_in"), S("stored")
        placed, hot, spread_made, summed, added = S("placed"), S("hot"), S("spread_made"), S("summed"), S("added")
        meaned, product_made, mixed = S("meaned"), S("product_made"), S("mixed")
        totalled, centred, squared, varied, rooted, inverted, normed = (S(n) for n in ("totalled", "centred", "squared", "varied", "rooted", "inverted", "normed"))
        turn_made, turn_out = S("turn_made"), S("turn_out")
        distance, taken, primed = sem(q("distance")), sem(q("slot_taken")), sem(q("primed"))
        if degrees:
            counted, clamped, inverse = S("counted"), S("clamped"), S("inverse")
        if relational:
            kind_hot, kinds_made, messages = S("kind_hot"), S("kinds_made"), S("messages")
            kinds_turned, kinds_out = sem(q("kinds_turned")), sem(q("kinds_out"))
        block = ctx.enter_context(nc.Block())
        lead = LEAD if relational else LEAD - 1
        norm_lead = 2 if relational else 1
        sums = W + C if degrees else W
        n_out = int(x_to is not None) + int(h_to is not None)

        def view(t):
            return t.rearrange("(b p c) d -> b p (c d)", p=128, c=C)

        def cd(ap):
            return ap.rearrange("p (c d) -> p c d", d=D)

        def wide(ap):
            return ap.unsqueeze(2).to_broadcast([128, C, D])

        def steps(eng, stages):
            for n in range(-lead, U):
                for stage, ahead in stages:
                    if n + ahead >= 0:
                        stage(n + ahead, (n + ahead) % U, (n + ahead) // U)
            with eng.Fori(1, eng.value_load(iters[0:1, 0:1], min_val=1, max_val=ITERS)) as i:
                for u in range(U):
                    for stage, ahead in stages:
                        stage(i * U + (u + ahead), (u + ahead) % U, i + (u + ahead) // U)

        def land(eng, sems, per_use, ahead):
            count = eng.value_load(iters[0:1, 0:1], min_val=1, max_val=ITERS)
            for u in range(U):
                eng.wait_ge(sems[u], (count + (ahead + U - 1 - u) // U) * 16 * per_use)
                eng.sem_inc(taken, 1)

        def before(u, r, back):
            return (u - back) % U, (r + 1 if u >= back else r)

        def store(eng):
            def stage(n, u, r):
                b = eng.value_load(ids[0:1, 1, bass.ds(n, 1)], min_val=0, max_val=NB)
                until(eng, normed[u] if norm else mixed[u], r + 1)
                for t, src in ((x_to, xn), (h_to, hn)):
                    if t is not None:
                        eng.dma_start(view(io[t])[bass.ds(b, 1), :, :].rearrange("b p w -> (b p) w"), src[:, u, :]).then_inc(stored[u], 16)
            return stage

        @block.sync
        def _(sp):
            def fetch_edges(n, u, r):
                until(sp, far_in[u], r * 16 * K)
                sp.sem_inc(taken, 1)
                until(sp, placed[u], r)
                sp.sem_inc(taken, 1)
                until(sp, hot[u], r * (2 if weighted else 1))
                sp.dma_start(edges[:, u, :, :].rearrange("p k w -> p (k w)"),
                             io["tab"][a][bass.ds(n * CAP, CAP), :].rearrange("(p k) w -> p (k w)", k=K)).then_inc(edges_in[u], 16)

            def fetch_block(t, dst, arrived, used):
                def stage(n, u, r):
                    b = sp.value_load(ids[0:1, 0, bass.ds(n, 1)], min_val=0, max_val=NB - 1)
                    until(sp, used[u], r)
                    sp.dma_start(dst[:, u, :], view(io[t])[bass.ds(b, 1), :, :].rearrange("b p w -> (b p) w")).then_inc(arrived[u], 16)
                return stage

            own_ahead, x_ahead = lead if relational else 5, norm_lead + 3
            steps(sp, [(fetch_edges, lead), *([(fetch_block(h_of, hb, own_in, turn_out), own_ahead)] if own else []),
                       *([(fetch_block(x_of, xb, x_in, mixed), x_ahead)] if x_of else []),
                       *([(store(sp), 0)] if relational else [])])
            if relational:
                land(sp, stored, n_out, 0)
            land(sp, edges_in, 1, lead)
            if own:
                land(sp, own_in, 1, own_ahead)
            if x_of:
                land(sp, x_in, 1, x_ahead)

        @block.gpsimd
        def _(pool):
            def gather(n, u, r):
                until(pool, edges_in[u], r * 16 + 16)
                pool.sem_inc(taken, 1)
                until(pool, kinds_made[u] if relational else spread_made[u], r)
                pool.sem_inc(taken, 1)
                for k in range(K):
                    nc.gpsimd.indirect_dma_start(
                        out=far[:, u, k, :], out_offset=None, in_=io[rows_of][0:NB * BLK, :],
                        in_offset=bass.IndirectOffsetOnAxis(ap=edges[:, u, k, 0:1].bitcast(i32), axis=0)).then_inc(far_in[u], 16)

            steps(pool, [(gather, lead)])
            land(pool, far_in, K, lead)

        @block.tensor
        def _(pe):
            def front(n, u, r):
                until(pe, placed[u], r + 1)
                until(pe, spread_made[u], r + 1)
                v, c = before(u, r, 2)
                until(pe, added[v], c)
                p = ps_sum[u % 2]
                for k in range(K):
                    mm = nc.tensor.matmul(p[:, 0:sums], place[:, u, k, :], spread[:, u, k, 0:sums], start=(k == 0), stop=(k == K - 1 and not relational))
                if relational:
                    until(pe, turn_out[u], r + 1)
                    for j in range(2):
                        mm = nc.tensor.matmul(p[:, j * 128:(j + 1) * 128], turned[:, u % 2, 2 + j, :], keepers[weights][:, 1, :],
                                              start=False, stop=False, skip_group_check=True)
                    mm = nc.tensor.matmul(p[:, 0:W], keepers["ones3"][:, :], keepers["zeros3"][:, :], start=False, stop=True)
                mm.then_inc(summed[u], 1)

            def turn(n, u, r):
                until(pe, own_in[u], (r + 1) * 16)
                v, c = before(u, r, 1)
                until(pe, turn_out[v], c)
                if sage:
                    until(pe, meaned[u], r + 1)
                for s, t in ((0, mean), (1, hb)) if sage else ((1, hb),):
                    for j in range(2):
                        tr = nc.tensor.transpose(ps_turn[:, 2 * s + j, :], t[:, u, j * 128:(j + 1) * 128], ident[:, :])
                tr.then_inc(turn_made[u], 1)

            def product(n, u, r):
                until(pe, turn_out[u], r + 1)
                v, c = before(u, r, 2)
                until(pe, mixed[v], c)
                for j in range(2):
                    half = ps_mix[u % 2][:, j * 128:(j + 1) * 128]
                    nc.tensor.matmul(half, keepers["ones3"][:, :], keepers[bias][:, j * 128:(j + 1) * 128], start=True, stop=False)
                    for s in range(2):
                        mm = nc.tensor.matmul(half, turned[:, u % 2, 2 * s + j, :], keepers[weights][:, s, :], start=False, stop=(s == 1))
                mm.then_inc(product_made[u], 1)

            def transpose(k):
                def stage(n, u, r):
                    if k == 0:
                        until(pe, kinds_made[u], r + 1)
                    if u * K + k >= 2 or not isinstance(n, int):
                        until(pe, kinds_out, n * K + k - 1)
                    for j in range(4):
                        t = nc.tensor.transpose(ps_kind[(u * K + k) % 2][:, j, :], by_kind[:, u % 2, k, j * 128:(j + 1) * 128], ident[:, :])
                    t.then_inc(kinds_turned, 1)
                return stage

            def multiply(k):
                def stage(n, u, r):
                    if k == 0:
                        v, c = before(u, r, 2)
                        until(pe, spread_made[v], c)
                    until(pe, kinds_out, n * K + k + 1)
                    for j in range(4):
                        mm = nc.tensor.matmul(ps_msg[u % 2][:, k * D:(k + 1) * D], kind_turned[:, (u * K + k) % 2, j, :],
                                              keepers["w_rel"][:, j, :], start=(j == 0), stop=(j == 3))
                    if k == K - 1:
                        mm.then_inc(messages[u], 1)
                return stage

            if relational:
                steps(pe, [(transpose(0), 7), (transpose(1), 7), (front, 5), (multiply(0), 7), (transpose(2), 7), (multiply(1), 7),
                           (turn, 6), (multiply(2), 7)])
            elif sage:
                steps(pe, [(product, 2), (turn, 3), (front, 5)])
            else:
                steps(pe, [(front, 5)])

        @block.scalar
        def _(act):
            def distances(n, u, r):
                until(act, edges_in[u], r * 16 + 16)
                for k in range(K):
                    d = nc.scalar.activation(apart[:, u % 2, k, :], iota[:, 0:128], ACT.Abs, bias=edges[:, u, k, 1:2])
                d.then_inc(distance, 1)

            def placing(n, u, r):
                until(act, summed[u], r)
                until(act, distance, n + 1)
                nc.scalar.activation(place[:, u, :, :], apart[:, u % 2, :, :], ACT.Relu, bias=1.0, scale=-1.0).then_inc(placed[u], 1)

            def squares(n, u, r):
                until(act, centred[u], r + 1)
                until(act, varied[u], r)
                nc.scalar.activation(sq[:, u, :], xc[:, u, :], ACT.Square).then_inc(squared[u], 1)

            def root(n, u, r):
                until(act, varied[u], r + 1)
                nc.scalar.activation(st[:, u, 2, :], st[:, u, 1, :], ACT.Sqrt, bias=eps[:, :], scale=1.0 / D).then_inc(rooted[u], 1)

            def kinds(k):
                def stage(n, u, r):
                    until(act, kinds_turned, n * K + k + 1)
                    s = (u * K + k) % 2
                    nc.scalar.activation(kind_turned[:, s, :, :], ps_kind[s][:, :, :], ACT.Copy).then_inc(kinds_out, 1)
                return stage

            def evacuate(n, u, r):
                until(act, turn_made[u], r + 1)
                if sage:
                    nc.scalar.activation(turned[:, u % 2, :, :], ps_turn[:, :, :], ACT.Copy).then_inc(turn_out[u], 1)
                else:
                    v, c = before(u, r, 2)
                    until(act, summed[v], c)
                    nc.scalar.activation(turned[:, u % 2, 2:4, :], ps_turn[:, 2:4, :], ACT.Copy, scale=fresh[:, bass.ds(n, 1)]).then_inc(turn_out[u], 1)

            def activate(n, u, r):
                until(act, product_made[u], r + 1)
                until(act, stored[u], r * 16 * n_out)
                nc.scalar.activation(hn[:, u, :], ps_mix[u % 2][:, 0:W], ACT.Relu).then_inc(mixed[u], 1)

            place_edge = [(distances, 6), (placing, 6)]
            if relational:
                steps(act, [(kinds(0), 7), (squares, 2), (kinds(1), 7), (root, 1), (distances, 6), (kinds(2), 7), (evacuate, 6), (placing, 6)])
            elif norm:
                steps(act, [(root, 0), (distances, 6), (squares, 1), (placing, 6), *([(evacuate, 3)] if sage else []), (store(act), 0)])
            elif sage:
                steps(act, [(activate, 1), *place_edge, (evacuate, 3), (store(act), 0)])
            else:
                steps(act, [*place_edge, (store(act), 0)])
            if not relational:
                land(act, stored, n_out, 0)

        @block.vector
        def _(dve):
            v = nc.vector

            def chunks(n, u, r):
                until(dve, edges_in[u], r * 16 + 16)
                until(dve, summed[u], r)
                v.tensor_tensor(spread[:, u, :, W:W + C], edges[:, u, :, 2:3].to_broadcast([128, K, C]),
                                iota[:, 0:C].unsqueeze(1).to_broadcast([128, K, C]), ALU.is_equal).then_inc(hot[u], 1)

            def weigh(n, u, r):
                until(dve, hot[u], 2 * r + 1)
                v.tensor_tensor(spread[:, u, :, W:W + C], spread[:, u, :, W:W + C], edges[:, u, :, 4:5].to_broadcast([128, K, C]), ALU.mult).then_inc(hot[u], 1)

            def spreading(k):
                def stage(n, u, r):
                    if k == 0:
                        until(dve, hot[u], (2 if weighted else 1) * (r + 1))
                        if relational:
                            until(dve, messages[u], r + 1)
                        else:
                            until(dve, far_in[u], (r + 1) * 16 * K)
                    rows = ps_msg[u % 2][:, k * D:(k + 1) * D] if relational else far[:, u, k, :]
                    s = v.tensor_tensor(cd(spread[:, u, k, 0:W]), rows.unsqueeze(1).to_broadcast([128, C, D]), wide(spread[:, u, k, W:W + C]), ALU.mult)
                    if k == K - 1:
                        s.then_inc(spread_made[u], 1)
                return stage

            def kinds_hot(n, u, r):
                until(dve, edges_in[u], r * 16 + 16)
                v.tensor_tensor(kind[:, u, :, :], edges[:, u, :, 3:4].to_broadcast([128, K, REL]),
                                iota[:, 0:REL].unsqueeze(1).to_broadcast([128, K, REL]), ALU.is_equal).then_inc(kind_hot[u], 1)

            def kinds(k):
                def stage(n, u, r):
                    if k == 0:
                        until(dve, kind_hot[u], r + 1)
                        until(dve, far_in[u], (r + 1) * 16 * K)
                        w, c = before(u, r, 2)
                        until(dve, messages[w], c)
                    s = v.tensor_tensor(by_kind[:, u % 2, k, :].rearrange("p (r d) -> p r d", d=D), far[:, u, k, :].unsqueeze(1).to_broadcast([128, REL, D]),
                                        kind[:, u, k, :].unsqueeze(2).to_broadcast([128, REL, D]), ALU.mult)
                    if k == K - 1:
                        s.then_inc(kinds_made[u], 1)
                return stage

            def count(n, u, r):
                until(dve, summed[u], r + 1)
                w, c = before(u, r, 1)
                until(dve, counted[w], c)
                v.scalar_tensor_tensor(out=deg[:, u, :], in0=deg[:, (u - 1) % U, :], scalar=keep[:, bass.ds(n, 1)],
                                       in1=ps_sum[u % 2][:, W:W + C], op0=ALU.mult, op1=ALU.add).then_inc(counted[u], 1)

            def add_up(n, u, r):
                until(dve, summed[u], r + 1)
                w, c = before(u, r, 1)
                until(dve, added[w], c)
                v.scalar_tensor_tensor(out=agg[:, u, :], in0=agg[:, (u - 1) % U, :], scalar=keep[:, bass.ds(n, 1)],
                                       in1=ps_sum[u % 2][:, 0:W], op0=ALU.mult, op1=ALU.add).then_inc(added[u], 1)

            def clamp(n, u, r):
                until(dve, counted[u], r + 1)
                v.tensor_scalar(st[:, u, 3, :], deg[:, u, :], 1.0, None, ALU.max).then_inc(clamped[u], 1)

            def invert(n, u, r):
                until(dve, clamped[u], r + 1)
                v.reciprocal(dinv[:, bass.ds(n, 1), :], st[:, u, 3, :].unsqueeze(1)).then_inc(inverse[u], 1)

            def average(n, u, r):
                if degrees:
                    until(dve, inverse[u], r + 1)
                until(dve, added[u], r + 1)
                v.tensor_tensor(cd(mean[:, u, :]), cd(agg[:, u, :]), wide(dinv[:, bass.ds(n, 1), :].rearrange("p a c -> p (a c)")), ALU.mult).then_inc(meaned[u], 1)

            def mix(n, u, r):
                until(dve, x_in[u], (r + 1) * 16)
                until(dve, stored[u], r * 16 * n_out)
                if sage:
                    until(dve, product_made[u], r + 1)
                else:
                    until(dve, added[u], r + 1)
                if own:
                    v.scalar_tensor_tensor(out=xn[:, u, :], in0=ps_mix[u % 2][:, 0:W] if sage else agg[:, u, :], scalar=0.0, in1=xb[:, u, :],
                                           op0=ALU.max, op1=ALU.add).then_inc(mixed[u], 1)
                else:
                    v.tensor_tensor(xn[:, u, :], agg[:, u, :], xb[:, u, :], ALU.add).then_inc(mixed[u], 1)

            def total(n, u, r):
                until(dve, mixed[u], r + 1)
                v.tensor_reduce(st[:, u, 0, :], cd(xn[:, u, :]), AX.X, ALU.add, negate=True).then_inc(totalled[u], 1)

            def centre(n, u, r):
                until(dve, totalled[u], r + 1)
                v.scalar_tensor_tensor(out=cd(xc[:, u, :]), in0=wide(st[:, u, 0, :]), scalar=1.0 / D, in1=cd(xn[:, u, :]),
                                       op0=ALU.mult, op1=ALU.add).then_inc(centred[u], 1)

            def variance(n, u, r):
                until(dve, squared[u], r + 1)
                v.tensor_reduce(st[:, u, 1, :], cd(sq[:, u, :]), AX.X, ALU.add).then_inc(varied[u], 1)

            def reciprocal(n, u, r):
                until(dve, rooted[u], r + 1)
                v.reciprocal(st[:, u, 3, :], st[:, u, 2, :]).then_inc(inverted[u], 1)

            def last(n, u, r):
                until(dve, inverted[u], r + 1)
                v.scalar_tensor_tensor(out=cd(hn[:, u, :]), in0=cd(xc[:, u, :]), scalar=0.0, in1=wide(st[:, u, 3, :]),
                                       op0=ALU.max, op1=ALU.mult).then_inc(normed[u], 1)

            v.memset(agg[:, U - 1, :], 0.0).then_inc(primed, 1)
            v.memset(deg[:, U - 1, :], 0.0).then_inc(primed, 1)
            until(dve, primed, 2)
            s0, s1, s2 = ((spreading(k), 5) for k in range(K))
            if degrees:
                steps(dve, [(chunks, 5), (count, 3), (add_up, 3), (clamp, 3), s0, (invert, 3), s1, (average, 3), s2])
            elif relational:
                steps(dve, [(kinds_hot, 7), (mix, 2), (chunks, 5), (total, 2), (add_up, 3), (centre, 2), (kinds(0), 7), (variance, 1),
                            (kinds(1), 7), (reciprocal, 0), (kinds(2), 7), s0, (last, 0), s1, s2])
            elif norm:
                steps(dve, [(mix, 1), (chunks, 5), (total, 1), (variance, 0), (centre, 1), (add_up, 3), s0,
                            *([(average, 3)] if sage else []), (reciprocal, 0), s1, (last, 0), s2])
            else:
                steps(dve, [(chunks, 5), (mix, 1), *([(weigh, 5)] if weighted else []), (add_up, 3), s0, s1, s2])


def load_weights(nc, io, keepers):
    with ExitStack() as ctx:
        sb, _, sem = tensors(nc, ctx)
        cleared, loaded, parts, moved, order = (sem(n) for n in ("weights_cleared", "weights_loaded", "bias_parts", "parts_moved", "bias_order"))
        bias, part, rest = sb("bias_row", [1, 2, W]), sb("bias_part", [1, 2, 3, W], bf16), sb("bias_rest", [1, 2, W])
        pairs = (("w_sage0", "sage0"), ("w_sage1", "sage1"), ("w_self", "own"))
        block = ctx.enter_context(nc.Block())

        @block.gpsimd
        def _(pool):
            for _, dst in pairs:
                nc.gpsimd.memset(keepers[dst][:, :, :], 0.0).then_inc(cleared, 1)

        @block.sync
        def _(sp):
            sp.dma_start(bias[:, 0, :], io["b0"].unsqueeze(0)).then_inc(loaded, 16)
            sp.dma_start(bias[:, 1, :], io["b1"].unsqueeze(0)).then_inc(loaded, 16)
            sp.wait_ge(loaded, 32)
            sp.wait_ge(cleared, len(pairs))
            for name, dst in pairs:
                for half in range(2):
                    own = slice(D * half, D * half + D)
                    sp.dma_start(keepers[dst][own, :, own], io[name].rearrange("s i o -> i s o")).then_inc(loaded, 16)
            for j in range(REL // 2):
                for half in range(2):
                    sp.dma_start(keepers["w_rel"][D * half:D * half + D, j, :], io["w_rel"][2 * j + half, :, :]).then_inc(loaded, 16)
            sp.wait_ge(parts, 2)
            for b in range(2):
                for k in range(3):
                    sp.dma_start(keepers[f"b{b}"][k:k + 1, :], part[:, b, k, :]).then_inc(moved, 16)
            sp.wait_ge(loaded, 16 * (2 + 2 * len(pairs) + REL))
            sp.wait_ge(moved, 16 * 6)

        @block.vector
        def _(dve):
            v = nc.vector
            v.memset(keepers["zeros3"][:, :], 0.0)
            v.memset(keepers["ones3"][:, :], 1.0).then_inc(parts, 1)
            dve.wait_ge(loaded, 32)
            v.tensor_copy(part[:, :, 0, :], bias[:, :, :]).then_inc(order, 1)
            dve.wait_ge(order, 1)
            v.tensor_tensor(rest[:, :, :], bias[:, :, :], part[:, :, 0, :], ALU.subtract).then_inc(order, 1)
            dve.wait_ge(order, 2)
            v.tensor_copy(part[:, :, 1, :], rest[:, :, :]).then_inc(order, 1)
            dve.wait_ge(order, 3)
            v.tensor_tensor(rest[:, :, :], rest[:, :, :], part[:, :, 1, :], ALU.subtract).then_inc(order, 1)
            dve.wait_ge(order, 4)
            v.tensor_copy(part[:, :, 2, :], rest[:, :, :]).then_inc(parts, 1)


def build(nc, io):
    with ExitStack() as ctx:
        def sb(name, shape, dt=fp32):
            return ctx.enter_context(nc.sbuf_tensor(name, shape, dt))

        for name in ("H0", "H1", "X1", "H3", "X2", "H4", "X3", "H5"):
            io[name] = nc.dram_tensor(name, (NROWS, D), fp32).ap()
        io["tab"] = [nc.dram_tensor(f"placed_{a}", (TROWS, PW), fp32).ap() for a in ("dst", "src")]
        keepers = {
            "iota": sb("iota", [128, NB + 1]), "ident": sb("ident", [128, 128]), "eps": sb("eps", [128, 1]),
            "keep": [sb(f"keep{a}", [128, J * 128]) for a in range(2)],
            "fresh": [sb(f"fresh{a}", [128, J * 128]) for a in range(2)],
            "ids": [sb(f"ids{a}", [128, 2, J * 128], i32) for a in range(2)],
            "iters": [sb(f"iters{a}", [128, 1], i32) for a in range(2)],
            "dinv": [sb("dinv", [128, J * 128, C])] * 2,
            "sage0": sb("w_sage0", [128, 2, 2 * D]), "sage1": sb("w_sage1", [128, 2, 2 * D]), "own": sb("w_own", [128, 2, 2 * D]),
            "w_rel": sb("w_rel", [128, REL // 2, D]), "ones3": sb("ones3", [3, 128], bf16), "zeros3": sb("zeros3", [3, W], bf16),
            "b0": sb("b0", [3, W], bf16), "b1": sb("b1", [3, W], bf16),
        }
        load_weights(nc, io, keepers)
        place_edges(nc, io, keepers)
        phase(nc, io, keepers, "A", 0, "H0", "H0", None, "sage0", "b0", None, "H1", degrees=True, norm=False)
        phase(nc, io, keepers, "B", 0, "H1", "H1", "x", "sage1", "b1", "X1", "H3")
        phase(nc, io, keepers, "C", 1, "H3", None, "X1", None, None, "X2", "H4")
        phase(nc, io, keepers, "D", 0, "H4", "H4", "X2", "own", None, "X3", "H5", relational=True)
        phase(nc, io, keepers, "E", 0, "H5", None, "X3", None, None, "out", None, weighted=True, norm=False)


def kernel(**inputs):
    import numpy as np
    import concourse.bacc as bacc
    from concourse.bass_utils import run_bass_kernel_spmd as run

    def padded(a, n, fill):
        out = np.full((n, *a.shape[1:]), fill, a.dtype)
        out[:len(a)] = a
        return out

    g = {k: np.asarray(v) for k, v in inputs.items()}
    arrays = {
        "x": padded(g["x"], NROWS, 0),
        "dst": padded(g["dst"].astype(np.int32), 128 * T, NB * BLK),
        "src": padded(g["src"].astype(np.int32), 128 * T, NB * BLK),
        "etype": padded(g["edge_type_8"].astype(np.int32), 128 * T, 0),
        "ew": padded(g["edge_weight"], 128 * T, 0),
        "w_sage0": np.stack([g["L0_gnn_W_neigh0"], g["L0_gnn_W_self0"]]),
        "w_sage1": np.stack([g["L0_gnn_W_neigh1"], g["L0_gnn_W_self1"]]),
        "w_self": np.ascontiguousarray(np.stack([g["L2_gnn_self_loop_w"].T, g["L2_gnn_self_loop_w"].T])),
        "w_rel": g["L2_gnn_weight"],
        "b0": np.tile(g["L0_gnn_b0"], C), "b1": np.tile(g["L0_gnn_b1"], C),
    }
    nc = bacc.Bacc("TRN2", target_bir_lowering=False, num_devices=1)
    io = {n: nc.dram_tensor(f"in_{n}", a.shape, i32 if a.dtype == np.int32 else fp32, kind="ExternalInput").ap() for n, a in arrays.items()}
    io["out"] = nc.dram_tensor("out_x", (NROWS, D), fp32, kind="ExternalOutput").ap()
    build(nc, io)
    r = run(nc, [{f"in_{n}": np.ascontiguousarray(a) for n, a in arrays.items()}], core_ids=[0])
    return r.results[0]["out_x"][:N]
```
